# Optimizing a Trainium2 kernel written in Bass

```python
import numpy as np
import jax
import jax.numpy as jnp

def _softmax(x, axis=-1):
    return jax.nn.softmax(x, axis=axis)
def _gelu(x):
    return jax.nn.gelu(x, approximate=True)
def _silu(x):
    return jax.nn.silu(x)
def _sigmoid(x):
    return jax.nn.sigmoid(x)
def _layernorm(x, axis=-1, eps=1e-5):
    m = jnp.mean(x, axis=axis, keepdims=True)
    v = jnp.var(x, axis=axis, keepdims=True)
    return (x - m) / jnp.sqrt(v + eps)
def _scatter_add(tgt, idx, src, axis=0):
    return tgt.at[idx].add(src)
def _segment_sum(src, seg, n):
    return jax.ops.segment_sum(src, seg, n)

kernel_name = 'mk_conv_seq_d2_conv_nchw256_7d9906'

def setup_inputs(seed: int = 0):
    np.random.seed(seed)
    _w = jnp.asarray
    def _rec_inputs():
        import jax
        import jax.numpy as jnp
        _gk = jax.random.key(seed)
        x = -0.0002928 + 1 * jax.random.normal(jax.random.fold_in(_gk, 1), (16, 256, 32, 32), jnp.float32)
        return x
    x = _rec_inputs()
    def _L0_conv_setup():
        import jax, jax.numpy as jnp
        import numpy as np
        C = 256
        NH = 4
        G = 8
        EPS = 1e-05

        def group_norm(x, weight, bias):
            B, Cc, H, W = x.shape
            xg = x.reshape(B, G, Cc // G, H, W)
            mean = xg.mean(axis=(2, 3, 4), keepdims=True)
            var = xg.var(axis=(2, 3, 4), keepdims=True)
            xg = (xg - mean) * jax.lax.rsqrt(var + EPS)
            xn = xg.reshape(B, Cc, H, W)
            return xn * weight[None, :, None, None] + bias[None, :, None, None]
        key = jax.random.key(seed)
        ks = jax.random.split(key, 7)
        B, H, W = (16, 32, 32)
        x = jax.random.normal(ks[0], (B, C, H, W), dtype=jnp.float32)
        n_weight = jnp.ones((C,), dtype=jnp.float32)
        n_bias = jnp.zeros((C,), dtype=jnp.float32)
        qkv_w = jax.random.normal(ks[1], (3 * C, C), dtype=jnp.float32) * C ** (-0.5)
        qkv_b = jnp.zeros((3 * C,), dtype=jnp.float32)
        p_w = jax.random.normal(ks[2], (C, C), dtype=jnp.float32) * C ** (-0.5)
        p_b = jnp.zeros((C,), dtype=jnp.float32)
        return {'x': x, 'n_weight': n_weight, 'n_bias': n_bias, 'qkv_w': qkv_w, 'qkv_b': qkv_b, 'p_w': p_w, 'p_b': p_b}
    _L0_conv_all = _L0_conv_setup()
    _L0_conv_in = {k: v for k, v in _L0_conv_all.items() if k in ('n_weight', 'n_bias', 'qkv_w', 'qkv_b', 'p_w', 'p_b', )}
    del _L0_conv_all

    def _L1_conv_setup():
        import jax, jax.numpy as jnp
        import numpy as np
        from jax import lax
        DIM = 256
        HEADS = 8
        WS = 15
        MLP_RATIO = 4
        HEAD_DIM = DIM // HEADS
        SCALE = HEAD_DIM ** (-0.5)
        EPS = 1e-06

        def _l2_normalize(t):
            n = jnp.sqrt(jnp.sum(t * t, axis=-1, keepdims=True))
            return t / jnp.maximum(n, 1e-12)

        def _self_attn(xw, wqkv, bqkv):
            Bw, N, C = xw.shape
            qkv = xw @ wqkv.T + bqkv
            q, k, v = jnp.split(qkv, 3, axis=-1)

            def heads(t):
                return t.reshape(Bw, N, HEADS, HEAD_DIM).transpose(0, 2, 1, 3)
            q, k, v = (heads(q), heads(k), heads(v))
            q = jax.nn.softplus(_l2_normalize(q))
            k = jax.nn.softplus(_l2_normalize(k))
            kv = jnp.einsum('bhnd,bhne->bhde', k, v) * SCALE
            ksum = jnp.sum(k, axis=2) + EPS
            norm = 1.0 / jnp.einsum('bhnd,bhd->bhn', q, ksum)
            out = jnp.einsum('bhnd,bhde,bhn->bhne', q, kv, norm)
            return out.transpose(0, 2, 1, 3).reshape(Bw, N, C)
        key = jax.random.key(seed)
        ks = jax.random.split(key, 9)
        B, H, W = (8, 128, 128)
        x = jax.random.normal(ks[0], (B, DIM, H, W), jnp.float32)
        conv_w = jax.random.normal(ks[1], (DIM, 1, 3, 3), jnp.float32) * 0.1
        conv_b = jax.random.normal(ks[2], (DIM,), jnp.float32) * 0.1
        wqkv = jax.random.normal(ks[3], (3 * DIM, DIM), jnp.float32) * DIM ** (-0.5)
        bqkv = jax.random.normal(ks[4], (3 * DIM,), jnp.float32) * 0.02
        wfc1 = jax.random.normal(ks[5], (MLP_RATIO * DIM, DIM), jnp.float32) * DIM ** (-0.5)
        bfc1 = jax.random.normal(ks[6], (MLP_RATIO * DIM,), jnp.float32) * 0.02
        wfc2 = jax.random.normal(ks[7], (DIM, MLP_RATIO * DIM), jnp.float32) * (MLP_RATIO * DIM) ** (-0.5)
        bfc2 = jax.random.normal(ks[8], (DIM,), jnp.float32) * 0.02
        return dict(x=x, conv_w=conv_w, conv_b=conv_b, wqkv=wqkv, bqkv=bqkv, wfc1=wfc1, bfc1=bfc1, wfc2=wfc2, bfc2=bfc2)
    _L1_conv_all = _L1_conv_setup()
    _L1_conv_in = {k: v for k, v in _L1_conv_all.items() if k in ('conv_w', 'conv_b', 'wqkv', 'bqkv', 'wfc1', 'bfc1', 'wfc2', 'bfc2', )}
    del _L1_conv_all

    return {
        "x": x,
        "L0_conv_n_weight": _L0_conv_in["n_weight"],
        "L0_conv_n_bias": _L0_conv_in["n_bias"],
        "L0_conv_qkv_w": _L0_conv_in["qkv_w"],
        "L0_conv_qkv_b": _L0_conv_in["qkv_b"],
        "L0_conv_p_w": _L0_conv_in["p_w"],
        "L0_conv_p_b": _L0_conv_in["p_b"],
        "L1_conv_conv_w": _L1_conv_in["conv_w"],
        "L1_conv_conv_b": _L1_conv_in["conv_b"],
        "L1_conv_wqkv": _L1_conv_in["wqkv"],
        "L1_conv_bqkv": _L1_conv_in["bqkv"],
        "L1_conv_wfc1": _L1_conv_in["wfc1"],
        "L1_conv_bfc1": _L1_conv_in["bfc1"],
        "L1_conv_wfc2": _L1_conv_in["wfc2"],
        "L1_conv_bfc2": _L1_conv_in["bfc2"],
    }

def reference(x, L0_conv_n_weight, L0_conv_n_bias, L0_conv_qkv_w, L0_conv_qkv_b, L0_conv_p_w, L0_conv_p_b, L1_conv_conv_w, L1_conv_conv_b, L1_conv_wqkv, L1_conv_bqkv, L1_conv_wfc1, L1_conv_bfc1, L1_conv_wfc2, L1_conv_bfc2):
    import jax
    import jax.numpy as jnp
    def _L0_conv_ref(x, n_weight, n_bias, qkv_w, qkv_b, p_w, p_b):
        import jax, jax.numpy as jnp
        import numpy as np
        C = 256
        NH = 4
        G = 8
        EPS = 1e-05

        def group_norm(x, weight, bias):
            B, Cc, H, W = x.shape
            xg = x.reshape(B, G, Cc // G, H, W)
            mean = xg.mean(axis=(2, 3, 4), keepdims=True)
            var = xg.var(axis=(2, 3, 4), keepdims=True)
            xg = (xg - mean) * jax.lax.rsqrt(var + EPS)
            xn = xg.reshape(B, Cc, H, W)
            return xn * weight[None, :, None, None] + bias[None, :, None, None]
        B, Cc, H, W = x.shape
        N = H * W
        dh = Cc // NH
        sc = dh ** (-0.5)
        xn = group_norm(x, n_weight, n_bias)
        xn_flat = xn.reshape(B, Cc, N)
        qkv = jnp.einsum('oc,bcn->bon', qkv_w, xn_flat) + qkv_b[None, :, None]
        qkv = qkv.reshape(B, 3, NH, dh, N)
        q, k, v = (qkv[:, 0], qkv[:, 1], qkv[:, 2])
        a = jax.nn.softmax(jnp.einsum('bhci,bhcj->bhij', q, k) * sc, axis=-1)
        o = jnp.einsum('bhij,bhcj->bhci', a, v).reshape(B, Cc, N)
        proj = jnp.einsum('oc,bcn->bon', p_w, o) + p_b[None, :, None]
        return x + proj.reshape(B, Cc, H, W)

    def _L1_conv_ref(x, conv_w, conv_b, wqkv, bqkv, wfc1, bfc1, wfc2, bfc2):
        import jax, jax.numpy as jnp
        import numpy as np
        from jax import lax
        DIM = 256
        HEADS = 8
        WS = 15
        MLP_RATIO = 4
        HEAD_DIM = DIM // HEADS
        SCALE = HEAD_DIM ** (-0.5)
        EPS = 1e-06

        def _l2_normalize(t):
            n = jnp.sqrt(jnp.sum(t * t, axis=-1, keepdims=True))
            return t / jnp.maximum(n, 1e-12)

        def _self_attn(xw, wqkv, bqkv):
            Bw, N, C = xw.shape
            qkv = xw @ wqkv.T + bqkv
            q, k, v = jnp.split(qkv, 3, axis=-1)

            def heads(t):
                return t.reshape(Bw, N, HEADS, HEAD_DIM).transpose(0, 2, 1, 3)
            q, k, v = (heads(q), heads(k), heads(v))
            q = jax.nn.softplus(_l2_normalize(q))
            k = jax.nn.softplus(_l2_normalize(k))
            kv = jnp.einsum('bhnd,bhne->bhde', k, v) * SCALE
            ksum = jnp.sum(k, axis=2) + EPS
            norm = 1.0 / jnp.einsum('bhnd,bhd->bhn', q, ksum)
            out = jnp.einsum('bhnd,bhde,bhn->bhne', q, kv, norm)
            return out.transpose(0, 2, 1, 3).reshape(Bw, N, C)
        pos = lax.conv_general_dilated(x, conv_w, window_strides=(1, 1), padding=((1, 1), (1, 1)), dimension_numbers=('NCHW', 'OIHW', 'NCHW'), feature_group_count=DIM)
        x = x + pos + conv_b[None, :, None, None]
        x = jnp.transpose(x, (0, 2, 3, 1))
        b, h, w, c = x.shape
        shortcut = x
        pad_b = -h % WS
        pad_r = -w % WS
        xp = jnp.pad(x, ((0, 0), (0, pad_b), (0, pad_r), (0, 0)))
        Hp, Wp = (h + pad_b, w + pad_r)
        nh, nw = (Hp // WS, Wp // WS)
        xw = xp.reshape(b, nh, WS, nw, WS, c).transpose(0, 1, 3, 2, 4, 5)
        xw = xw.reshape(b * nh * nw, WS * WS, c)
        aw = _self_attn(xw, wqkv, bqkv)
        xr = aw.reshape(b, nh, nw, WS, WS, c).transpose(0, 1, 3, 2, 4, 5).reshape(b, Hp, Wp, c)
        xr = xr[:, :h, :w, :]
        x = xr + shortcut
        hmid = x @ wfc1.T + bfc1
        x = x + (hmid @ wfc2.T + bfc2)
        return jnp.transpose(x, (0, 3, 1, 2))

    def _gn(v, G=32, eps=1e-5):
        B_, C_, H_, W_ = v.shape
        g = v.reshape(B_, G, C_ // G, H_, W_)
        m = jnp.mean(g, axis=(2, 3, 4), keepdims=True)
        s = jnp.var(g, axis=(2, 3, 4), keepdims=True)
        return ((g - m) / jnp.sqrt(s + eps)).reshape(v.shape)

    def _ln_c(v, eps=1e-6):
        m = jnp.mean(v, axis=1, keepdims=True)
        s = jnp.var(v, axis=1, keepdims=True)
        return (v - m) / jnp.sqrt(s + eps)

    def _ln_t(v, eps=1e-5):
        m = jnp.mean(v, axis=-1, keepdims=True)
        s = jnp.var(v, axis=-1, keepdims=True)
        return (v - m) / jnp.sqrt(s + eps)

    def _to_tokens(v):
        B_, C_, H_, W_ = v.shape
        return v.reshape(B_, C_, H_ * W_).transpose(0, 2, 1)
    def _from_tokens(t, like):
        B_, C_, H_, W_ = like.shape
        return t.transpose(0, 2, 1).reshape(B_, C_, H_, W_)

    x = _L0_conv_ref(x, L0_conv_n_weight, L0_conv_n_bias, L0_conv_qkv_w, L0_conv_qkv_b, L0_conv_p_w, L0_conv_p_b)
    x = _L1_conv_ref(x, L1_conv_conv_w, L1_conv_conv_b, L1_conv_wqkv, L1_conv_bqkv, L1_conv_wfc1, L1_conv_bfc1, L1_conv_wfc2, L1_conv_bfc2)
    return x


_drawn_inputs = setup_inputs


def setup_inputs(seed=0):
    import zlib

    import numpy as np

    out = dict(_drawn_inputs(seed))
    spreads = {'L0_conv_n_weight': (1.0, 0.2),
     'L0_conv_n_bias': (0.0, 0.1),
     'L0_conv_qkv_b': (0.0, 0.1),
     'L0_conv_p_b': (0.0, 0.1)}
    factors = {'L1_conv_bqkv': 8.0, 'L1_conv_bfc1': 4.199, 'L1_conv_bfc2': 4.45}
    for name, (base, spread) in spreads.items():
        noise = np.random.default_rng([zlib.crc32(name.encode()), seed]).standard_normal(out[name].shape)
        drawn = base * np.exp(spread * noise) if base else spread * noise
        out[name] = jnp.asarray(drawn.astype(out[name].dtype))
    for name, factor in factors.items():
        out[name] = (out[name] * factor).astype(out[name].dtype)
    return out
```

```python
import math
from contextlib import ExitStack

import concourse.bass as bass
from concourse import mybir

P = 128
F32 = mybir.dt.float32
F32R = mybir.dt.float32r
ALU = mybir.AluOpType
ACT = mybir.ActivationFunctionType
AX = mybir.AxisListType

RING = 4
LAG = 2
HALF = 512
DMA = 16
SLOTS = 3


def channel_tiles(ap):
    return ap.rearrange("(t p) n -> p t n", p=P)



HEADS0 = 4
MAX_TILES = {2: (0, 1), 3: (2, 3), 4: (4, 5), 5: (6, 7)}
MAX_TURNED = 6


def products0(first, last):
    order = []
    for h in range(HEADS0):
        for j in range(8):
            order.append(("scores", h, j))
            if not (last and h == 3):
                order += [("max", (h + 1) % HEADS0, i) for i in MAX_TILES.get(j, ())]
                if j == MAX_TURNED:
                    order.append(("maxT", (h + 1) % HEADS0))
            if h == 0 and j in (1, 2):
                order.append(("v", j - 1))
            if h == 0 and j in (4, 6):
                order.append(("qk", 1, j // 2 - 2))
            if h == 2 and j in (0, 1) and not last:
                order.append(("group", j == 1))
            if h == 2 and j in (5, 7) and not last:
                order.append(("qk", 0, j // 2 - 2))
            if h == 3 and j in (0, 1) or h == 1 and j in (0, 1) and not first:
                order.append(("proj", h // 2, j))
            if j == 3 and not (first and h == 0):
                order.append(("sum", h))
    return order


HEAD_ORDER = ([("group", False), ("group", True), ("qk", 0, 0), ("qk", 0, 1)]
              + [("max", 0, i) for i in range(8)] + [("maxT", 0)])
TAIL_ORDER = [("sum", 0), ("proj", 0, 0), ("proj", 0, 1)]


def needed(count):
    return not isinstance(count, int) or count > 0


class Product:

    def __init__(self, tile, full, free, turn, loops):
        self.tile, self.full, self.free, self.turn, self.loops = tile, full, free, turn, loops

    @property
    def filled(self):
        return self.loops + (self.turn + 1)

    @property
    def emptied(self):
        return self.loops + self.turn


class Slots:

    def __init__(self, slots, order, before, loops=0, per=0):
        assert len(set(order)) == len(order) and per % len(slots) == 0
        self.slots, self.loops = slots, loops * (per // len(slots))
        self.at = {name: before + k for k, name in enumerate(order)}

    def __getitem__(self, name):
        turn, slot = divmod(self.at[name], len(self.slots))
        return Product(*self.slots[slot], turn, self.loops)


def layer0(nc, x, vectors, qkv_wT, p_wT, y):
    B, C, N = x.shape
    CT = C // P
    JT = N // P
    HD = C // HEADS0
    GROUP = C // 8
    VH = HEADS0 * 2 * HD
    SCALE = float(HD) ** -0.5
    EPS = 1e-5
    assert (C, N) == (256, 1024)

    PER = len(products0(False, False))
    BEFORE_FIRST = len(HEAD_ORDER)
    BEFORE_MID = BEFORE_FIRST + len(products0(True, False))
    BEFORE_LAST = BEFORE_MID + (B - 2) * PER
    BEFORE_TAIL = BEFORE_LAST + len(products0(False, True))

    with ExitStack() as ctx:
        def sb(name, shape, dt=F32):
            return ctx.enter_context(nc.sbuf_tensor(name, shape, dt))

        def sem(name):
            return ctx.enter_context(nc.semaphore(name))

        qkv_u, qkv_l = sb("qkv_u", [P, CT, 3 * C], F32R), sb("qkv_l", [P, CT, 3 * C], F32R)
        pw_u, pw_l = sb("pw_u", [P, CT, C], F32R), sb("pw_l", [P, CT, C], F32R)
        vecs = sb("vecs0", [P, 6 * CT])
        gnw, gnb, pb = (vecs[:, i * CT:(i + 1) * CT] for i in range(3))
        qkv_bias = vecs[:, 3 * CT:]
        out_bias = sb("out_bias", [P, CT])
        ident = sb("ident0", [P, P])
        group_mean = sb("group_mean", [P, P])
        ones_r = sb("ones_r", [P, P], F32R)
        block_rows = sb("block_rows", [JT, JT, P])
        xt = sb("xt", [P, CT, N])
        yt = sb("yt", [P, CT, N])
        xn_u, xn_l = sb("xn_u", [P, CT, N], F32R), sb("xn_l", [P, CT, N], F32R)
        xn_f = sb("xn_f", [P, N])
        stats, mv = sb("stats", [P, CT, 2, 6]), sb("mv", [P, CT, 2])
        gmean, dev, spread, gvar, lnvar, rstd, newton, gn_a, gn_c = (
            sb(n, [P, CT]) for n in ("gmean", "dev", "spread", "gvar", "lnvar", "rstd", "newton", "gn_a", "gn_c"))
        qk_u, qk_l = sb("qk_u", [P, 2, N], F32R), sb("qk_l", [P, 2, N], F32R)
        key1, key2 = sb("key1", [P, 2, N], F32R), sb("key2", [P, 2, N], F32R)
        qry1, qry2 = sb("qry1", [P, 2, N], F32R), sb("qry2", [P, 2, N], F32R)
        v_ul = sb("v_ul", [P, JT, HEADS0, 2, HD], F32R)
        neg_max = sb("neg_max", [P, JT])
        p_f = sb("p_f", [P, 2, N])
        p_u, p_l = sb("p_u", [P, RING, N], F32R), sb("p_l", [P, RING, N], F32R)
        psums = sb("psums", [P, 2, N])
        ps_u, ps_l = sb("ps_u", [P, N], F32R), sb("ps_l", [P, N], F32R)
        lnsum, rec = sb("lnsum", [P, N]), sb("rec", [P, N])
        o_low = sb("o_low", [HD, N])
        o_f, o_n = sb("o_f", [P, N]), sb("o_n", [P, N])
        o_u, o_l = sb("o_u", [P, N], F32R), sb("o_l", [P, N], F32R)
        qkv_f = p_f[:].rearrange("p a n -> p (a n)")[:, 0:CT * 3 * C].rearrange("p (t o) -> p t o", t=CT)
        pw_f = psums[:].rearrange("p a n -> p (a n)")[:, 0:CT * C].rearrange("p (t o) -> p t o", t=CT)

        av = ctx.enter_context(nc.psum_tensor("av", [P, 2 * HALF], F32))
        slots = [(ctx.enter_context(nc.psum_tensor(f"slot{i}", [P, 2 * HALF], F32)),
                  sem(f"slot_full{i}"), sem(f"slot_free{i}")) for i in range(SLOTS)]
        head_slots = Slots(slots, HEAD_ORDER, 0)
        tail_slots = Slots(slots, TAIL_ORDER, BEFORE_TAIL)

        (weights_in, consts_made, zeros_made, weights_split, bias_made, v_bias_full, x_in, y_begun, y_out, gn_made,
         rstd_ready, xn_u_ready, xn_f_ready, xn_l_ready, qk_u_ready, v_u_ready, p_u_ready, p_l_ready, p_added,
         p_used, av_free, o_low_ready, ps_u_ready, ps_l_ready, rec_ready, o_n_ready, o_u_ready, o_l_ready) = (
            sem(n) for n in (
             "weights_in", "consts_made", "zeros_made", "weights_split", "bias_made", "v_bias_full", "x_in", "y_begun",
             "y_out", "gn_made", "rstd_ready", "xn_u_ready", "xn_f_ready", "xn_l_ready", "qk_u_ready", "v_u_ready",
             "p_u_ready", "p_l_ready", "p_added", "p_used", "av_free", "o_low_ready", "ps_u_ready", "ps_l_ready",
             "rec_ready", "o_n_ready", "o_u_ready", "o_l_ready"))
        stacked = [sem("stacked0"), sem("stacked1")]
        const_step, shift_made = sem("const_step"), sem("shift_made")
        stats_waited, waited = sem("stats_waited"), sem("waited")
        GN_OPS = 16

        def for_images(eng, image):
            image(0, Slots(slots, products0(True, False), BEFORE_FIRST), first=True)
            with eng.Fori(1, B - 1) as b:
                image(b, Slots(slots, products0(False, False), BEFORE_MID - PER, b, PER))
            image(B - 1, Slots(slots, products0(False, True), BEFORE_LAST), last=True)

        halves = [slice(0, HALF), slice(HALF, 2 * HALF)]
        block = ctx.enter_context(nc.Block())

        @block.sync
        def _(sp):
            sp.dma_start(xt[:], channel_tiles(x[0])).then_inc(x_in, DMA)
            sp.dma_start(vecs[:], vectors).then_inc(weights_in, DMA)
            sp.dma_start(qkv_f, channel_tiles(qkv_wT)).then_inc(weights_in, DMA)
            sp.dma_start(pw_f, channel_tiles(p_wT)).then_inc(weights_in, DMA)

            def stack(b, h):
                s, rows = h % 2, slice(HD * (h % 2), HD * (h % 2) + HD)
                if needed(8 * (4 * b + h - 1)):
                    sp.wait_ge(p_u_ready, 8 * (4 * b + h - 1))
                top, low = slice(0, HD), slice(HD, P)
                for dst, src in ((qry1[top, s, :], qk_u[rows, 0, :]), (key1[top, s, :], qk_u[rows, 1, :]),
                                 (qry1[low, s, :], qk_u[rows, 0, :]), (key1[low, s, :], qk_l[rows, 1, :]),
                                 (key2[top, s, :], qk_u[rows, 1, :]), (qry2[top, s, :], qk_l[rows, 0, :])):
                    sp.dma_start(dst.bitcast(F32), src.bitcast(F32)).then_inc(stacked[s], DMA)

            sp.wait_ge(zeros_made, 1)
            it = head_slots["qk", 0, 0]
            sp.wait_ge(it.free, it.filled)
            sp.sem_inc(waited, 1)
            it = head_slots["qk", 0, 1]
            sp.wait_ge(it.free, it.filled)
            sp.sem_inc(waited, 1)
            stack(0, 0)

            def image(b, sl, first=False, last=False):
                stack(b, 1)
                it = sl["qk", 1, 0]
                sp.wait_ge(it.free, it.filled)
                sp.sem_inc(waited, 1)
                it = sl["qk", 1, 1]
                sp.wait_ge(it.free, it.filled)
                sp.sem_inc(waited, 1)
                stack(b, 2)
                if not first:
                    it = sl["proj", 0, 0]
                    sp.wait_ge(it.free, it.filled)
                    sp.sem_inc(waited, 1)
                    it = sl["proj", 0, 1]
                    sp.wait_ge(it.free, it.filled)
                    sp.sem_inc(waited, 1)
                    sp.dma_start(channel_tiles(y[b - 1]), yt[:]).then_inc(y_out, DMA)
                if not last:
                    coming = channel_tiles(x[b + 1])
                    sp.wait_ge(y_begun, CT * (b + 1))
                    sp.dma_start(xt[:], coming).then_inc(x_in, DMA)
                stack(b, 3)
                if not last:
                    it = sl["qk", 0, 0]
                    sp.wait_ge(it.free, it.filled)
                    sp.sem_inc(waited, 1)
                    it = sl["qk", 0, 1]
                    sp.wait_ge(it.free, it.filled)
                    sp.sem_inc(waited, 1)
                    stack(b + 1, 0)

            for_images(sp, image)
            for m in range(CT):
                it = tail_slots["proj", 0, m]
                sp.wait_ge(it.free, it.filled)
            sp.dma_start(channel_tiles(y[B - 1]), yt[:]).then_inc(y_out, DMA)
            sp.wait_ge(y_out, DMA * B)

        @block.tensor
        def _(pe):
            def product(out, left, right):
                terms = [(l, r) for (lu, ll), (ru, rl) in zip(left, right) for l, r in ((lu, ru), (lu, rl), (ll, ru))]
                for n, (l, r) in enumerate(terms):
                    mm = nc.tensor.matmul(out, l, r, start=(n == 0), stop=(n == len(terms) - 1))
                return mm

            def group(sl, images, second):
                pe.wait_ge(gn_made, GN_OPS * (images - 1) + (9 if second else 6))
                to = sl["group", second]
                if needed(to.emptied):
                    pe.wait_ge(to.free, to.emptied)
                out = to.tile
                nc.tensor.matmul(out[:, 0:CT], group_mean[:], spread[:] if second else mv[:, :, 0],
                                 start=True, stop=True).then_inc(to.full, 1)

            def qk(sl, images, pair, what):
                pe.wait_ge(xn_l_ready, CT * images)
                to = sl["qk", pair, what]
                if needed(to.emptied):
                    pe.wait_ge(to.free, to.emptied)
                out = to.tile
                o = what * C + pair * P
                for n in halves:
                    mm = product(out[:, n], [(qkv_u[:, k, o:o + P], qkv_l[:, k, o:o + P]) for k in range(CT)],
                                 [(xn_u[:, k, n], xn_l[:, k, n]) for k in range(CT)])
                mm.then_inc(to.full, 1)

            def values(sl, u):
                to = sl["v", u]
                if needed(to.emptied):
                    pe.wait_ge(to.free, to.emptied)
                out = to.tile
                for i in range(4):
                    j = slice((4 * u + i) * P, (4 * u + i + 1) * P)
                    mm = product(out[:, i * C:(i + 1) * C], [(xn_u[:, k, j], xn_l[:, k, j]) for k in range(CT)],
                                 [(qkv_u[:, k, 2 * C:], qkv_l[:, k, 2 * C:]) for k in range(CT)])
                mm.then_inc(to.full, 1)

            def row_scores(sl, b, h, i):
                if i == 0:
                    pe.wait_ge(stacked[h % 2], 6 * DMA * (2 * b + h // 2 + 1))
                to = sl["max", h % HEADS0, i]
                if needed(to.emptied):
                    pe.wait_ge(to.free, to.emptied)
                out = to.tile
                for n in halves:
                    mm = nc.tensor.matmul(out[:, n], qry1[:, h % 2, i * P:(i + 1) * P], key1[:, h % 2, n],
                                          start=True, stop=True)
                mm.then_inc(to.full, 1)

            def turn_max(sl, h):
                for i in range(5, 8):
                    it = sl["max", h, i]
                    pe.wait_ge(it.free, it.filled)
                to = sl["maxT", h]
                if needed(to.emptied):
                    pe.wait_ge(to.free, to.emptied)
                out = to.tile
                nc.tensor.transpose(out[0:JT, 0:P], neg_max[:], ident[:]).then_inc(to.full, 1)

            def scores(sl, h, j):
                s, jj = h % 2, slice(j * P, (j + 1) * P)
                to = sl["scores", h, j]
                if needed(to.emptied):
                    pe.wait_ge(to.free, to.emptied)
                out = to.tile
                for n in halves:
                    nc.tensor.matmul(out[:, n], key1[:, s, jj], qry1[:, s, n], start=True, stop=False)
                for n in halves:
                    mm = nc.tensor.matmul(out[:, n], key2[:, s, jj], qry2[:, s, n], start=False, stop=True)
                mm.then_inc(to.full, 1)

            def weigh(b, h, j, g):
                if j == 0:
                    if needed(4 * b + h):
                        pe.wait_ge(av_free, 4 * b + h)
                pe.wait_ge(p_l_ready, 32 * b + 8 * h + j + 1)
                r = g % RING
                for n in halves:
                    nc.tensor.matmul(av[:, n], v_ul[:, j, h, :, :].rearrange("p a d -> p (a d)"), p_u[:, r, n],
                                     start=(j == 0), stop=False, skip_group_check=True)
                for n in halves:
                    mm = nc.tensor.matmul(av[0:HD, n], v_ul[:, j, h, 0, :], p_l[:, r, n],
                                          start=False, stop=(j == JT - 1), skip_group_check=True)
                mm.then_inc(p_used, 1)

            def prob_sums(sl, heads, h):
                pe.wait_ge(ps_l_ready, heads)
                to = sl["sum", h]
                if needed(to.emptied):
                    pe.wait_ge(to.free, to.emptied)
                out = to.tile
                for n in halves:
                    nc.tensor.matmul(out[:, n], ones_r[:], ps_u[:, n], start=True, stop=False)
                    mm = nc.tensor.matmul(out[:, n], ones_r[:], ps_l[:, n], start=False, stop=True)
                mm.then_inc(to.full, 1)

            def project(sl, pairs, pair, at, m):
                pe.wait_ge(o_l_ready, pairs)
                to = sl["proj", at, m]
                if needed(to.emptied):
                    pe.wait_ge(to.free, to.emptied)
                out = to.tile
                mm_ = slice(m * P, (m + 1) * P)
                for n in halves:
                    mm = product(out[:, n], [(pw_u[:, pair, mm_], pw_l[:, pair, mm_])], [(o_u[:, n], o_l[:, n])])
                mm.then_inc(to.full, 1)

            pe.wait_ge(weights_in, 3 * DMA)
            for m in range(CT):
                for k in range(CT):
                    mm = nc.tensor.matmul(av[:, m:m + 1], pw_f[:, k, m * P:(m + 1) * P],
                                          qkv_bias[:, 2 * CT + k:2 * CT + k + 1], start=(k == 0), stop=(k == CT - 1))
            mm.then_inc(v_bias_full, 1)
            pe.wait_ge(consts_made, 4)
            group(head_slots, 1, False)
            group(head_slots, 1, True)
            pe.wait_ge(weights_split, 4)
            qk(head_slots, 1, 0, 0)
            qk(head_slots, 1, 0, 1)
            for i in range(JT):
                row_scores(head_slots, 0, 0, i)
            turn_max(head_slots, 0)
            it = head_slots["maxT", 0]
            pe.wait_ge(it.free, it.filled)
            pe.wait_ge(bias_made, 1)

            def image(b, sl, first=False, last=False):
                for h in range(HEADS0):
                    for j in range(JT):
                        scores(sl, h, j)
                        if not (last and h == 3):
                            for i in MAX_TILES.get(j, ()):
                                row_scores(sl, b, h + 1, i)
                            if j == MAX_TURNED:
                                turn_max(sl, (h + 1) % HEADS0)
                        if h == 0 and j in (1, 2):
                            values(sl, j - 1)
                        if j >= LAG:
                            if h == 0 and j == LAG:
                                it = sl["v", 0]
                                pe.wait_ge(it.free, it.filled)
                                it = sl["v", 1]
                                pe.wait_ge(it.free, it.filled)
                            weigh(b, h, j - LAG, 8 * h + j - LAG)
                        elif not (first and h == 0):
                            weigh_before(b, h, j)
                        if h == 0 and j in (4, 6):
                            qk(sl, b + 1, 1, j // 2 - 2)
                        if h == 2 and j in (0, 1) and not last:
                            group(sl, b + 2, j == 1)
                        if h == 2 and j in (5, 7) and not last:
                            qk(sl, b + 2, 0, j // 2 - 2)
                        if h == 3 and j in (0, 1):
                            project(sl, 2 * b + 1, 0, 1, j)
                        if h == 1 and j in (0, 1) and not first:
                            project(sl, 2 * b, 1, 0, j)
                        if j == 3 and not (first and h == 0):
                            prob_sums(sl, 4 * b + h, h)
                        if j == 7 and not (last and h == 3):
                            it = sl["maxT", (h + 1) % HEADS0]
                            pe.wait_ge(it.free, it.filled)

            def weigh_before(b, h, j):
                jj = JT - LAG + j
                if h == 0:
                    weigh(b - 1, HEADS0 - 1, jj, 8 * (HEADS0 - 1) + jj)
                else:
                    weigh(b, h - 1, jj, 8 * (h - 1) + jj)

            for_images(pe, image)
            for j in range(LAG):
                weigh(B - 1, HEADS0 - 1, JT - LAG + j, 8 * (HEADS0 - 1) + JT - LAG + j)
            prob_sums(tail_slots, 4 * B, 0)
            project(tail_slots, 2 * B, 1, 0, 0)
            project(tail_slots, 2 * B, 1, 0, 1)

        @block.scalar
        def _(act):
            def copy_qk(sl, pairs, pair, what):
                for s in range(2):
                    if needed(6 * DMA * (pairs - 1)):
                        act.wait_ge(stacked[s], 6 * DMA * (pairs - 1))
                it = sl["qk", pair, what]
                act.wait_ge(it.full, it.filled)
                src = it.tile
                nc.scalar.activation(qk_u[:, what, :], src[:], ACT.Identity,
                                     bias=qkv_bias[:, CT * what + pair:CT * what + pair + 1]).then_inc(qk_u_ready, 1)

            def copy_v(sl, b, u):
                if needed(32 * b - 4 + 4 * u):
                    act.wait_ge(p_used, 32 * b - 4 + 4 * u)
                it = sl["v", u]
                act.wait_ge(it.full, it.filled)
                src = it.tile
                nc.scalar.copy(v_ul[:, 4 * u:4 * u + 4, :, 0, :],
                               src[:].rearrange("p (j h d) -> p j h d", j=4, h=HEADS0)).then_inc(v_u_ready, 1)

            def probs(b, sl, h, j):
                g = 8 * h + j
                it = sl["scores", h, j]
                act.wait_ge(it.full, it.filled)
                src = it.tile
                if needed(32 * b + g - 1):
                    act.wait_ge(p_l_ready, 32 * b + g - 1)
                added = {0: -1, 1: 0, 2: 1}.get(j, j - 2)
                if needed(7 * (4 * b + h) + added):
                    act.wait_ge(p_added, 7 * (4 * b + h) + added)
                nc.scalar.activation(p_f[:, g % 2, :], src[:], ACT.Exp, scale=SCALE).then_inc(it.free, 1)
                it = sl["scores", h, j]
                act.wait_ge(it.free, it.filled)
                if needed(32 * b + g - RING + 1):
                    act.wait_ge(p_used, 32 * b + g - RING + 1)
                nc.scalar.copy(p_u[:, g % RING, :], p_f[:, g % 2, :]).then_inc(p_u_ready, 1)

            def lower_half(heads):
                act.wait_ge(p_used, 8 * heads)
                if needed(heads - 1):
                    act.wait_ge(av_free, heads - 1)
                nc.scalar.copy(o_low[:], av[HD:P, :]).then_inc(o_low_ready, 1)

            def reciprocal_sums(sl, heads, h):
                it = sl["sum", h]
                act.wait_ge(it.full, it.filled)
                src = it.tile
                nc.scalar.activation(lnsum[:], src[:], ACT.Ln).then_inc(it.free, 1)
                it = sl["sum", h]
                act.wait_ge(it.free, it.filled)
                if needed(heads - 1):
                    act.wait_ge(o_n_ready, heads - 1)
                nc.scalar.activation(rec[:], lnsum[:], ACT.Exp, scale=-1.0).then_inc(rec_ready, 1)

            def rough_rstd(images):
                act.wait_ge(gn_made, GN_OPS * (images - 1) + 10)
                nc.scalar.activation(lnvar[:], gvar[:], ACT.Ln).then_inc(rstd_ready, 1)
                act.wait_ge(rstd_ready, 2 * images - 1)
                nc.scalar.activation(rstd[:], lnvar[:], ACT.Exp, scale=-0.5).then_inc(rstd_ready, 1)

            def normalise(images, t):
                act.wait_ge(gn_made, GN_OPS * images)
                for out, s in ((xn_u[:, t, :], xn_u_ready), (xn_f[:], xn_f_ready)):
                    if s is xn_f_ready:
                        if needed(CT * (images - 1) + t):
                            act.wait_ge(xn_l_ready, CT * (images - 1) + t)
                    nc.scalar.activation(out, xt[:, t, :], ACT.Identity, scale=gn_a[:, t:t + 1],
                                         bias=gn_c[:, t:t + 1]).then_inc(s, 1)

            def begin_y(b):
                if needed(DMA * b):
                    act.wait_ge(y_out, DMA * b)
                act.wait_ge(bias_made, 1)
                for t in range(CT):
                    nc.scalar.activation(yt[:, t, :], xt[:, t, :], ACT.Identity,
                                         bias=out_bias[:, t:t + 1]).then_inc(y_begun, 1)

            nc.scalar.preload_act_table_set("natural_log_exp_and_others")
            act.wait_ge(weights_in, 3 * DMA)
            rough_rstd(1)
            act.wait_ge(x_in, DMA)
            normalise(1, 0)
            normalise(1, 1)
            copy_qk(head_slots, 1, 0, 0)
            copy_qk(head_slots, 1, 0, 1)
            act.wait_ge(weights_split, 4)

            def image(b, sl, first=False, last=False):
                for h in range(HEADS0):
                    for j in range(JT):
                        probs(b, sl, h, j)
                        if h == 0 and j in (1, 2):
                            copy_v(sl, b, j - 1)
                        if j == 1 and not (first and h == 0):
                            lower_half(4 * b + h)
                        if h == 0 and j in (4, 6):
                            copy_qk(sl, 2 * b + 2, 1, j // 2 - 2)
                        if h == 1 and j == 3:
                            begin_y(b)
                        if h == 2 and not last:
                            if j == 1:
                                rough_rstd(b + 2)
                            if j in (2, 3):
                                if j == 2:
                                    it = sl["qk", 1, 1]
                                    act.wait_ge(it.free, it.filled)
                                normalise(b + 2, j - 2)
                            if j in (5, 7):
                                copy_qk(sl, 2 * b + 3, 0, j // 2 - 2)
                        if j == 3 and not (first and h == 0):
                            reciprocal_sums(sl, 4 * b + h, h)

            for_images(act, image)
            lower_half(4 * B)
            reciprocal_sums(tail_slots, 4 * B, 0)

        @block.vector
        def _(dve):
            def lower_qk(sl, pairs, pair, what):
                dve.wait_ge(qk_u_ready, 2 * (pairs - 1) + what + 1)
                it = sl["qk", pair, what]
                dve.wait_ge(it.full, it.filled)
                src = it.tile
                nc.vector.scalar_tensor_tensor(
                    out=qk_l[:, what, :], in0=src[:], scalar=qkv_bias[:, CT * what + pair:CT * what + pair + 1],
                    in1=qk_u[:, what, :].bitcast(F32), op0=ALU.add, op1=ALU.subtract).then_inc(it.free, 1)

            def lower_v(sl, b, u):
                dve.wait_ge(v_u_ready, 2 * b + u + 1)
                it = sl["v", u]
                dve.wait_ge(it.full, it.filled)
                src = it.tile
                nc.vector.tensor_tensor(
                    v_ul[:, 4 * u:4 * u + 4, :, 1, :], src[:].rearrange("p (j h d) -> p j h d", j=4, h=HEADS0),
                    v_ul[:, 4 * u:4 * u + 4, :, 0, :].bitcast(F32), ALU.subtract).then_inc(it.free, 1)

            def lower_probs(b, sl, h, j):
                g = 8 * h + j
                dve.wait_ge(p_u_ready, 32 * b + g + 1)
                nc.vector.tensor_tensor(p_l[:, g % RING, :], p_f[:, g % 2, :], p_u[:, g % RING, :].bitcast(F32),
                                        ALU.subtract).then_inc(p_l_ready, 1)

            def row_max(sl, h, i):
                it = sl["max", h, i]
                dve.wait_ge(it.full, it.filled)
                src = it.tile
                nc.vector.tensor_reduce(neg_max[:, i:i + 1], src[:], AX.X, ALU.max, negate=True).then_inc(it.free, 1)

            def place_max(sl, h):
                it = sl["maxT", h]
                dve.wait_ge(it.full, it.filled)
                src = it.tile
                nc.vector.tensor_tensor(
                    qry2[HD:HD + JT, h % 2, :].rearrange("p (c n) -> p c n", c=JT),
                    src[0:JT, 0:P].unsqueeze(1).broadcast_to([JT, JT, P]), block_rows[:], ALU.mult).then_inc(it.free, 1)

            def upper_sums(heads, s):
                dve.wait_ge(p_added, 7 * heads)
                if needed(heads - 1):
                    dve.wait_ge(rec_ready, heads - 1)
                nc.vector.tensor_copy(ps_u[:], psums[:, s, :]).then_inc(ps_u_ready, 1)

            def join_halves(heads, h):
                dve.wait_ge(o_low_ready, heads)
                if needed(heads - 2):
                    dve.wait_ge(o_n_ready, heads - 2)
                nc.vector.tensor_tensor(o_f[HD * (h % 2):HD * (h % 2) + HD, :], av[0:HD, :], o_low[:],
                                        ALU.add).then_inc(av_free, 1)

            def upper_out(pairs):
                dve.wait_ge(o_n_ready, 2 * pairs)
                nc.vector.tensor_copy(o_u[:], o_n[:]).then_inc(o_u_ready, 1)

            def add_projection(sl, at, m, begun):
                dve.wait_ge(y_begun, begun)
                it = sl["proj", at, m]
                dve.wait_ge(it.full, it.filled)
                src = it.tile
                nc.vector.tensor_tensor(yt[:, m, :], src[:], yt[:, m, :], ALU.add).then_inc(it.free, 1)

            def gn(instruction):
                instruction.then_inc(gn_made, 1)

            def image_stats(images):
                n = GN_OPS * (images - 1)
                dve.wait_ge(x_in, DMA * images)
                for t in range(CT):
                    for half in range(2):
                        gn(nc.vector.bn_stats(stats[:, t, half, :], xt[:, t, halves[half]]))
                dve.wait_ge(gn_made, n + 4)
                dve.sem_inc(stats_waited, 1)
                for t in range(CT):
                    gn(nc.vector.bn_aggr(mv[:, t, :], stats[:, t, :, :]))

            def group_spread(sl, images):
                n = GN_OPS * (images - 1)
                it = sl["group", False]
                dve.wait_ge(it.full, it.filled)
                src = it.tile
                nc.vector.tensor_copy(gmean[:], src[:, 0:CT]).then_inc(it.free, 1)
                it = sl["group", False]
                dve.wait_ge(it.free, it.filled)
                gn(nc.vector.tensor_tensor(dev[:], mv[:, :, 0], gmean[:], ALU.subtract))
                dve.wait_ge(gn_made, n + 7)
                gn(nc.vector.tensor_tensor(newton[:], dev[:], dev[:], ALU.mult))
                dve.wait_ge(gn_made, n + 8)
                gn(nc.vector.tensor_tensor(spread[:], newton[:], mv[:, :, 1], ALU.add))

            def group_var(sl, images):
                it = sl["group", True]
                dve.wait_ge(it.full, it.filled)
                src = it.tile
                gn(nc.vector.tensor_scalar(gvar[:], src[:, 0:CT], EPS, None, ALU.add))
                dve.wait_ge(gn_made, GN_OPS * (images - 1) + 10)
                dve.sem_inc(it.free, 1)

            def group_affine(images):
                n = GN_OPS * (images - 1)
                dve.wait_ge(rstd_ready, 2 * images)
                gn(nc.vector.tensor_tensor(newton[:], rstd[:], rstd[:], ALU.mult))
                dve.wait_ge(gn_made, n + 11)
                gn(nc.vector.tensor_tensor(dev[:], newton[:], gvar[:], ALU.mult))
                dve.wait_ge(gn_made, n + 12)
                gn(nc.vector.tensor_scalar(newton[:], dev[:], -0.5, 1.5, ALU.mult, ALU.add))
                dve.wait_ge(gn_made, n + 13)
                gn(nc.vector.tensor_tensor(dev[:], newton[:], rstd[:], ALU.mult))
                dve.wait_ge(gn_made, n + 14)
                gn(nc.vector.tensor_tensor(gn_a[:], dev[:], gnw, ALU.mult))
                dve.wait_ge(gn_made, n + 15)
                nc.vector.tensor_tensor(newton[:], gmean[:], gn_a[:], ALU.mult).then_inc(shift_made, 1)
                dve.wait_ge(shift_made, images)
                gn(nc.vector.tensor_tensor(gn_c[:], gnb, newton[:], ALU.subtract))

            dve.wait_ge(weights_in, 3 * DMA)
            nc.vector.tensor_copy(qkv_u[:], qkv_f).then_inc(weights_split, 1)
            nc.vector.tensor_copy(pw_u[:], pw_f).then_inc(weights_split, 1)
            dve.wait_ge(weights_split, 2)
            nc.vector.tensor_tensor(qkv_l[:], qkv_f, qkv_u[:].bitcast(F32), ALU.subtract).then_inc(weights_split, 1)
            nc.vector.tensor_tensor(pw_l[:], pw_f, pw_u[:].bitcast(F32), ALU.subtract).then_inc(weights_split, 1)
            dve.wait_ge(v_bias_full, 1)
            nc.vector.tensor_tensor(out_bias[:], av[:, 0:CT], pb, ALU.add).then_inc(bias_made, 1)
            image_stats(1)
            group_spread(head_slots, 1)
            group_var(head_slots, 1)
            group_affine(1)
            lower_qk(head_slots, 1, 0, 0)
            lower_qk(head_slots, 1, 0, 1)
            for i in range(JT):
                row_max(head_slots, 0, i)
            place_max(head_slots, 0)

            def image(b, sl, first=False, last=False):
                for h in range(HEADS0):
                    for j in range(JT):
                        if j == 2 and not (first and h == 0):
                            join_halves(4 * b + h, (h - 1) % HEADS0)
                        if not (last and h == 3):
                            for i in MAX_TILES.get(j, ()):
                                row_max(sl, (h + 1) % HEADS0, i)
                            if j == MAX_TURNED:
                                place_max(sl, (h + 1) % HEADS0)
                        lower_probs(b, sl, h, j)
                        if h == 0 and j in (1, 2):
                            lower_v(sl, b, j - 1)
                        if h == 0 and j in (4, 6):
                            lower_qk(sl, 2 * b + 2, 1, j // 2 - 2)
                        if h == 1 and j == 7 and not last:
                            image_stats(b + 2)
                        if h == 2 and not last:
                            if j == 0:
                                group_spread(sl, b + 2)
                            if j == 1:
                                group_var(sl, b + 2)
                            if j == 2:
                                group_affine(b + 2)
                            if j in (5, 7):
                                lower_qk(sl, 2 * b + 3, 0, j // 2 - 2)
                        if h == 3 and j in (0, 1):
                            add_projection(sl, 1, j, CT * (b + 1))
                        if h == 1 and j in (0, 1) and not first:
                            add_projection(sl, 0, j, CT * b)
                        if not (first and h == 0):
                            if j == 1:
                                upper_sums(4 * b + h, (h - 1) % 2)
                            if j == 6 and h % 2 == 0:
                                upper_out(2 * b + h // 2)

            for_images(dve, image)
            upper_sums(4 * B, 1)
            join_halves(4 * B, HEADS0 - 1)
            upper_out(2 * B)
            add_projection(tail_slots, 0, 0, CT * B)
            add_projection(tail_slots, 0, 1, CT * B)

        @block.gpsimd
        def _(pool):
            def add_probs(b, sl, h, j):
                n = 7 * (4 * b + h) + j - 1
                if j == 1:
                    if needed(4 * b + h - 1):
                        pool.wait_ge(ps_l_ready, 4 * b + h - 1)
                else:
                    pool.wait_ge(p_added, n)
                it = sl["scores", h, j]
                pool.wait_ge(it.free, it.filled)
                acc = psums[:, h % 2, :]
                g = 8 * h + j
                nc.gpsimd.tensor_tensor(acc, p_f[:, (g - 1) % 2, :] if j == 1 else acc, p_f[:, g % 2, :],
                                        ALU.add).then_inc(p_added, 1)

            def lower_sums(heads, s):
                pool.wait_ge(ps_u_ready, heads)
                nc.gpsimd.tensor_tensor(ps_l[:], psums[:, s, :], ps_u[:].bitcast(F32), ALU.subtract).then_inc(ps_l_ready, 1)

            def divide(heads, h, added):
                rows = slice(HD * (h % 2), HD * (h % 2) + HD)
                pool.wait_ge(p_added, added)
                pool.wait_ge(av_free, heads)
                pool.wait_ge(rec_ready, heads)
                if h % 2 == 0:
                    if needed((heads - 1) // 2):
                        pool.wait_ge(o_l_ready, (heads - 1) // 2)
                nc.gpsimd.tensor_tensor(o_n[rows, :], o_f[rows, :], rec[rows, :], ALU.mult).then_inc(o_n_ready, 1)
                pool.wait_ge(o_n_ready, heads)

            def lower_out(pairs):
                pool.wait_ge(o_u_ready, pairs)
                nc.gpsimd.tensor_tensor(o_l[:], o_n[:], o_u[:].bitcast(F32), ALU.subtract).then_inc(o_l_ready, 1)

            def lower_normed(images, t):
                n = CT * (images - 1) + t
                pool.wait_ge(xn_f_ready, n + 1)
                nc.gpsimd.tensor_tensor(xn_l[:, t, :], xn_f[:], xn_u[:, t, :].bitcast(F32),
                                        ALU.subtract).then_inc(xn_l_ready, 1)

            made = [0]

            def const(instruction):
                made[0] += 1
                instruction.then_inc(const_step, 1)
                pool.wait_ge(const_step, made[0])

            const(nc.gpsimd.memset(ident[:], 0.0))
            const(nc.gpsimd.affine_select(out=ident[:], in_=ident[:], compare_op=ALU.not_equal, fill=1.0, base=0,
                                          pattern=[[-1, P]], channel_multiplier=1))
            const(nc.gpsimd.memset(group_mean[:], 1.0 / GROUP))
            gm = group_mean[:].rearrange("p (g c) -> p g c", c=GROUP)
            const(nc.gpsimd.affine_select(out=gm, in_=gm, compare_op=ALU.is_ge, fill=0.0, base=0,
                                          pattern=[[-GROUP, P // GROUP], [0, GROUP]], channel_multiplier=1))
            const(nc.gpsimd.affine_select(out=gm, in_=gm, compare_op=ALU.is_ge, fill=0.0, base=GROUP - 1,
                                          pattern=[[GROUP, P // GROUP], [0, GROUP]], channel_multiplier=-1))
            const(nc.gpsimd.memset(block_rows[:], 0.0))
            const(nc.gpsimd.affine_select(out=block_rows[:], in_=block_rows[:], compare_op=ALU.not_equal, fill=1.0,
                                          base=0, pattern=[[-1, JT], [0, P]], channel_multiplier=1))
            const(nc.gpsimd.memset(xn_f[:], 1.0))
            const(nc.gpsimd.tensor_copy(ones_r[:], xn_f[:, 0:P]))
            const(nc.gpsimd.memset(o_n[:], 0.0))
            for s in range(2):
                const(nc.gpsimd.tensor_copy(key2[HD:P, s, :], o_n[HD:P, :]))
                const(nc.gpsimd.tensor_copy(qry2[HD:P, s, :], o_n[HD:P, :]))
                const(nc.gpsimd.tensor_copy(key2[HD:HD + JT, s, :], xn_f[HD:HD + JT, :]))
            pool.sem_inc(consts_made, 4)
            pool.sem_inc(zeros_made, 1)
            lower_normed(1, 0)
            lower_normed(1, 1)
            pool.wait_ge(bias_made, 1)

            def image(b, sl, first=False, last=False):
                for h in range(HEADS0):
                    for j in range(JT):
                        if j:
                            add_probs(b, sl, h, j)
                        if not (first and h == 0):
                            if j == 1:
                                lower_sums(4 * b + h, (h - 1) % 2)
                            if j == 4:
                                divide(4 * b + h, (h - 1) % HEADS0, 7 * (4 * b + h) + 4)
                            if j == 6 and h % 2 == 0:
                                lower_out(2 * b + h // 2)
                        if h == 2 and j in (2, 3) and not last:
                            lower_normed(b + 2, j - 2)

            for_images(pool, image)
            lower_sums(4 * B, 1)
            pool.wait_ge(ps_l_ready, 4 * B)
            divide(4 * B, HEADS0 - 1, 7 * 4 * B)
            lower_out(2 * B)



HEADS1 = 8
WS = 15
SIDE = 32
FULL = 2 * WS
EDGE = SIDE - FULL
WHOLE, CUT = 4, [WS * EDGE] * 4 + [EDGE * EDGE]
WINDOWS = [(w * WS * WS, WS * WS) for w in range(WHOLE)]
for size in CUT:
    WINDOWS.append((sum(WINDOWS[-1]), size))
EDGES = WINDOWS[WHOLE][0]
TILES = [(w, WINDOWS[w][0] + i * 113, 113 - i) for w in range(WHOLE) for i in range(2)] + [(None, EDGES, sum(CUT))]
SLOTS1 = 4


def orders(image, windows):
    image = image.rearrange("p (r c) -> p r c", c=SIDE)
    for band in range(2):
        yield (image[:, band * WS:(band + 1) * WS, 0:FULL].rearrange("p r (w c) -> p w r c", c=WS),
               windows[:, band * 2 * WS * WS:(band + 1) * 2 * WS * WS].rearrange("p (w r c) -> p w r c", w=2, c=WS))
    right = windows[:, EDGES:EDGES + FULL * EDGE]
    yield image[:, 0:FULL, FULL:SIDE], right.rearrange("p (r c) -> p r c", c=EDGE)
    low = windows[:, EDGES + FULL * EDGE:EDGES + 2 * FULL * EDGE]
    yield (image[:, FULL:SIDE, 0:FULL].rearrange("p r (w c) -> p w r c", c=WS),
           low.rearrange("p (w r c) -> p w r c", w=2, c=WS))
    yield (image[:, FULL:SIDE, FULL:SIDE],
           windows[:, EDGES + 2 * FULL * EDGE:].rearrange("p (r c) -> p r c", c=EDGE))


ORDERS = 5


def finish_order():
    return [("den", 0), ("den", 1), ("num", 0), ("num", 1)]


def products1(first):
    order = [("q", 0), ("q", 1)]
    order += [("kv", u) for u in range((len(TILES) + 1) // 2)]
    order += [("norm", 0), ("norm", 1)]
    if not first:
        order += finish_order()
    order += [("state", u) for u in range(3)]
    if not first:
        order += [("mlp", 0), ("mlp", 1)]
    return order


def layer1(nc, y, vectors, taps, wqkvT, kv_bias, fc1, fc2T, out):
    B, C, N = y.shape
    CT = C // P
    NW = len(WINDOWS)
    NT = len(TILES)
    HD = C // HEADS1
    F = fc1.shape[0]
    FT = F // P
    SCALE = float(HD) ** -0.5
    EPS = 1e-6
    NORM_MIN = 1e-12
    LIFT = 2.0 ** 20
    PAD = P - 1
    assert (C, N, SIDE * SIDE) == (256, 1024, 1024)

    U = len(products1(False))
    U0 = len(products1(True))
    assert 2 * U % SLOTS1 == 0

    with ExitStack() as ctx:
        def sb(name, shape, dt=F32):
            return ctx.enter_context(nc.sbuf_tensor(name, shape, dt))

        def sem(name):
            return ctx.enter_context(nc.semaphore(name))

        w_u, w_l = sb("w_u", [P, CT, 3 * C], F32R), sb("w_l", [P, CT, 3 * C], F32R)
        m_u, m_l = sb("m_u", [P, CT, C], F32R), sb("m_l", [P, CT, C], F32R)
        vecs = sb("vecs1", [P, 3 * CT + FT])
        conv_b, q_bias, fc2_b, fc1_b = (vecs[:, a:b] for a, b in ((0, CT), (CT, 2 * CT), (2 * CT, 3 * CT), (3 * CT, 3 * CT + FT)))
        tap = sb("tap", [P, CT, 9])
        centre = sb("centre", [P, CT])
        mlp_bias = sb("mlp_bias", [P, CT])
        kvb = sb("kvb", [P, 2 * C])
        head_ones = sb("head_ones", [P, P])
        head_scale = sb("head_scale", [P, P])
        unlift = sb("unlift", [P, 1])

        cut_mask = sb("cut_mask", [P, len(CUT)])

        y_in = sb("y_in", [P, CT, N])
        y_pad = sb("y_pad", [P, CT, SIDE + 2, SIDE + 2])
        x1 = sb("x1", [P, CT, N])
        x1w = [sb("x1wa", [P, CT, N]), sb("x1wb", [P, CT, N])]
        x1_u, x1_l = sb("x1_u", [P, CT, N], F32R), sb("x1_l", [P, CT, N], F32R)
        q_f = sb("q_f", [P, CT, N])
        q_w = sb("q_w", [P, CT, N])
        q_s = sb("q_s", [P, CT, N])
        k_in = sb("k_in", [P, NT, C])
        k_w = sb("k_w", [P, NT, C])
        v1 = sb("v1", [P, NT, CT, P + 2])
        v_cut = sb("v_cut", [P, len(CUT), CT, P + 2])
        ksq, kln, krn, knw = (sb(n, [P, NT * HEADS1]) for n in ("ksq", "kln", "krn", "knw"))
        kv, ks = sb("kv", [P, CT * NW, P]), sb("ks", [P, CT * NW, P])
        x2 = sb("x2", [P, CT, N])
        res = sb("res", [P, CT, N])
        x2_u, x2_l = sb("x2_u", [P, CT, N], F32R), sb("x2_l", [P, CT, N], F32R)

        def flat(tile, width):
            return tile[:].rearrange("p a n -> p (a n)")[:, 0:width]

        w_f = flat(q_f, CT * 3 * C).rearrange("p (t o) -> p t o", t=CT)
        fc1_f = flat(x2, FT * C).rearrange("p (t o) -> p t o", t=FT)
        fc2_f = flat(res, FT * C).rearrange("p (t o) -> p t o", t=FT)

        slots = [(ctx.enter_context(nc.psum_tensor(f"slot1_{i}", [P, 2 * HALF], F32)),
                  sem(f"slot1_full{i}"), sem(f"slot1_free{i}")) for i in range(SLOTS1)]
        early = [tile for tile, _, _ in slots]
        tail_slots = Slots(slots, finish_order() + [("mlp", 0), ("mlp", 1)], U0 + (B - 1) * U)
        (w_in, c_step, consts, w_split, mlp_made, w_ready, y_loaded, padded, centred, x1_u_ready,
         x1_l_ready, q_f_ready, q_clamped, q_rn, q_n, q_step, q_s_ready, k_added, k_step, k_rn, k_n, k_s_ready,
         rec_ready, ordered, v_added, v_split, x2_ready, x2_u_ready, x2_l_ready, out_ready, out_sent, kv_ready, v_inited) = (
            sem("l1_" + n) for n in (
             "w_in", "c_step", "consts", "w_split", "mlp_made", "w_ready", "y_loaded", "padded", "centred", 
             "x1_u_ready", "x1_l_ready", "q_f_ready", "q_clamped", "q_rn", "q_n", "q_step", "q_s_ready",
             "k_added", "k_step", "k_rn", "k_n", "k_s_ready", "rec_ready", "ordered", "v_added", "v_split", "x2_ready", "x2_u_ready",
             "x2_l_ready", "out_ready", "out_sent", "kv_ready", "v_inited"))

        tapped = [sem("l1_tapped0"), sem("l1_tapped1")]

        def for_images(eng, image):
            image(0, 0, Slots(slots, products1(True), 0), first=True)
            image(1, 1, Slots(slots, products1(False), U0))
            with eng.Fori(1, B // 2 - 1) as i:
                for p in range(2):
                    image(i * 2 + p, p, Slots(slots, products1(False), U0 + U + p * U - 2 * U, i, 2 * U))
            before = U0 + U + (B // 2 - 2) * 2 * U
            image(B - 2, 0, Slots(slots, products1(False), before))
            image(B - 1, 1, Slots(slots, products1(False), before + U), last=True)

        halves = [slice(0, HALF), slice(HALF, 2 * HALF)]

        def image_view(ap):
            return ap.rearrange("p (r c) -> p r c", c=SIDE)

        block = ctx.enter_context(nc.Block())

        @block.sync
        def _(sp):
            for dst, src in ((vecs[:], vectors), (tap[:], taps.rearrange("(t p) k -> p t k", p=P)),
                             (kvb[:], kv_bias.unsqueeze(0).broadcast_to([P, 2 * C])),
                             (w_f, channel_tiles(wqkvT)), (fc1_f, channel_tiles(fc1)), (fc2_f, channel_tiles(fc2T))):
                sp.dma_start(dst, src).then_inc(w_in, DMA)
            sp.wait_ge(v_inited, 1)
            sp.dma_start(k_in[PAD:P, NT - 1, :], kv_bias[0:C].unsqueeze(0)).then_inc(w_in, DMA)
            sp.dma_start(v1[PAD:P, NT - 1, :, 0:P],
                         kv_bias[C:].rearrange("(t d) -> t d", t=CT).unsqueeze(0)).then_inc(w_in, DMA)

            def load(b):
                if needed(CT * b):
                    sp.wait_ge(centred, CT * b)
                sp.dma_start(y_in[:], channel_tiles(y[b])).then_inc(y_loaded, DMA)

            def store(b):
                sp.wait_ge(out_ready, ORDERS * CT * (b + 1))
                sp.dma_start(channel_tiles(out[b]), res[:]).then_inc(out_sent, DMA)

            load(0)

            def image(b, p, sl, first=False, last=False):
                if not last:
                    load(b + 1)
                if not first:
                    store(b - 1)

            for_images(sp, image)
            store(B - 1)
            sp.wait_ge(out_sent, DMA * B)

        @block.tensor
        def _(pe):
            def product(o, left, right):
                terms = [(l, r) for (lu, ll), (ru, rl) in zip(left, right) for l, r in ((lu, ru), (lu, rl), (ll, ru))]
                for n, (l, r) in enumerate(terms):
                    mm = nc.tensor.matmul(o, l, r, start=(n == 0), stop=(n == len(terms) - 1))
                return mm

            pe.wait_ge(w_in, 8 * DMA)
            for m in range(CT):
                for f in range(FT):
                    mm = nc.tensor.matmul(early[m][:, 0:C], fc1_f[:, f, m * P:(m + 1) * P], fc2_f[:, f, :],
                                          start=(f == 0), stop=(f == FT - 1))
            for m in range(CT):
                for f in range(FT):
                    mm = nc.tensor.matmul(early[2][:, m:m + 1], fc2_f[:, f, m * P:(m + 1) * P], fc1_b[:, f:f + 1],
                                          start=(f == 0), stop=(f == FT - 1))
            mm.then_inc(mlp_made, 1)
            pe.wait_ge(w_ready, 1)
            pe.wait_ge(consts, 1)

            def q_products(sl, t):
                to = sl["q", t]
                if needed(to.emptied):
                    pe.wait_ge(to.free, to.emptied)
                o = to.tile
                m = slice(t * P, (t + 1) * P)
                for n in halves:
                    mm = product(o[:, n], [(w_u[:, k, m], w_l[:, k, m]) for k in range(CT)],
                                 [(x1_u[:, k, n], x1_l[:, k, n]) for k in range(CT)])
                mm.then_inc(to.full, 1)

            def kv_products(sl, u):
                to = sl["kv", u]
                if needed(to.emptied):
                    pe.wait_ge(to.free, to.emptied)
                o = to.tile
                for i, (_, first_, tokens) in enumerate(TILES[2 * u:2 * u + 2]):
                    n = slice(first_, first_ + tokens)
                    mm = product(o[0:tokens, i * HALF:(i + 1) * HALF],
                                 [(x1_u[:, k, n], x1_l[:, k, n]) for k in range(CT)],
                                 [(w_u[:, k, C:], w_l[:, k, C:]) for k in range(CT)])
                mm.then_inc(to.full, 1)

            def square_sums(sl, b, t):
                pe.wait_ge(q_f_ready, 2 * CT * b + 2 * t + 2)
                to = sl["norm", t]
                if needed(to.emptied):
                    pe.wait_ge(to.free, to.emptied)
                o = to.tile
                for n in halves:
                    mm = nc.tensor.matmul(o[:, n], head_ones[:], q_w[:, t, n], start=True, stop=True)
                mm.then_inc(to.full, 1)

            def state(sl, b, u):
                pe.wait_ge(k_s_ready, b + 1)
                pe.wait_ge(v_split, b + 1)
                to = sl["state", u]
                if needed(to.emptied):
                    pe.wait_ge(to.free, to.emptied)
                o = to.tile
                for cell in range(6 * u, 6 * u + 6):
                    t, w = divmod(cell, NW)
                    at_ = cell % 6 // 3 * HALF + cell % 3 * (P + 2)
                    mine = ([(n, v1[:, n, t, :]) for n in (2 * w, 2 * w + 1)] if w < WHOLE
                            else [(NT - 1, v_cut[:, w - WHOLE, t, :])])
                    for i, (n, v) in enumerate(mine):
                        mm = nc.tensor.matmul(o[:, at_:at_ + P + 2], k_w[:, n, t * P:(t + 1) * P], v,
                                              start=(i == 0), stop=(i == len(mine) - 1))
                mm.then_inc(to.full, 1)

            def attend(sl, images):
                pe.wait_ge(q_s_ready, CT * images)
                pe.wait_ge(kv_ready, 9 * images)
                for name, table in (("den", ks), ("num", kv)):
                    for t in range(CT):
                        to = sl[name, t]
                        if needed(to.emptied):
                            pe.wait_ge(to.free, to.emptied)
                        o = to.tile
                        for w, (at_, tokens) in enumerate(WINDOWS):
                            cuts = sorted({at_, min(max(HALF, at_), at_ + tokens), at_ + tokens})
                            for a, b in zip(cuts, cuts[1:]):
                                mm = nc.tensor.matmul(o[:, a:b], table[:, t * NW + w, :], q_s[:, t, a:b],
                                                      start=True, stop=True)
                        mm.then_inc(to.full, 1)

            def mlp(sl, images, m):
                pe.wait_ge(x2_l_ready, CT * images)
                to = sl["mlp", m]
                if needed(to.emptied):
                    pe.wait_ge(to.free, to.emptied)
                o = to.tile
                mm_ = slice(m * P, (m + 1) * P)
                for n in halves:
                    mm = product(o[:, n], [(m_u[:, k, mm_], m_l[:, k, mm_]) for k in range(CT)],
                                 [(x2_u[:, k, n], x2_l[:, k, n]) for k in range(CT)])
                mm.then_inc(to.full, 1)

            def image(b, p, sl, first=False, last=False):
                pe.wait_ge(x1_l_ready, CT * (b + 1))
                for t in range(CT):
                    q_products(sl, t)
                for u in range((NT + 1) // 2):
                    kv_products(sl, u)
                for t in range(CT):
                    square_sums(sl, b, t)
                if not first:
                    attend(sl, b)
                for u in range(3):
                    state(sl, b, u)
                if not first:
                    for m in range(CT):
                        mlp(sl, b, m)

            for_images(pe, image)
            attend(tail_slots, B)
            for m in range(CT):
                mlp(tail_slots, B, m)

        @block.scalar
        def _(act):
            def prepare(b, p):
                act.wait_ge(y_loaded, DMA * (b + 1))
                for t in range(CT):
                    if needed(8 * b):
                        act.wait_ge(tapped[t], 8 * b)
                    nc.scalar.copy(y_pad[:, t, 1:SIDE + 1, 1:SIDE + 1], image_view(y_in[:, t, :])).then_inc(padded, 1)
                    if needed(ORDERS * (CT * (b - 1) + t + 1)):
                        act.wait_ge(ordered, ORDERS * (CT * (b - 1) + t + 1))
                    nc.scalar.activation(x1[:, t, :], y_in[:, t, :], ACT.Identity, scale=centre[:, t:t + 1],
                                         bias=conv_b[:, t:t + 1]).then_inc(centred, 1)

            def upper_x1(b, p, sl):
                for t in range(CT):
                    act.wait_ge(tapped[t], 8 * (b + 1))
                    if needed(CT * (b - 1)):
                        act.wait_ge(x2_ready, CT * (b - 1))
                    for image_, windows in orders(x1[:, t, :], x1w[p][:, t, :]):
                        nc.scalar.copy(windows, image_).then_inc(ordered, 1)
                    act.wait_ge(ordered, ORDERS * (CT * b + t + 1))
                    if sl is not None:
                        it = sl["kv", (NT - 1) // 2]
                        act.wait_ge(it.free, it.filled)
                    nc.scalar.copy(x1_u[:, t, :], x1w[p][:, t, :]).then_inc(x1_u_ready, 1)

            def q_parts(sl, b, t):
                it = sl["q", t]
                act.wait_ge(it.full, it.filled)
                src = it.tile
                if needed(CT * b):
                    act.wait_ge(q_n, CT * b)
                nc.scalar.activation(q_f[:, t, :], src[:], ACT.Identity, bias=q_bias[:, t:t + 1]).then_inc(q_f_ready, 1)
                if needed(CT * b):
                    act.wait_ge(q_s_ready, CT * b)
                nc.scalar.activation(q_w[:, t, :], src[:], ACT.Square, bias=q_bias[:, t:t + 1]).then_inc(q_f_ready, 1)
                act.wait_ge(q_f_ready, 2 * CT * b + 2 * t + 2)
                act.sem_inc(it.free, 1)

            def q_rnorm(b, t):
                n = 2 * (CT * b + t)
                act.wait_ge(q_clamped, CT * b + t + 1)
                nc.scalar.activation(q_w[:, t, :], q_w[:, t, :], ACT.Ln, scale=LIFT).then_inc(q_rn, 1)
                act.wait_ge(q_rn, n + 1)
                nc.scalar.activation(q_w[:, t, :], q_w[:, t, :], ACT.Exp, scale=-0.5, bias=unlift[:]).then_inc(q_rn, 1)

            def q_softplus(b, t):
                act.wait_ge(q_n, CT * b + t + 1)
                nc.scalar.activation(q_w[:, t, :], q_w[:, t, :], ACT.Exp).then_inc(q_step, 1)
                act.wait_ge(q_step, CT * b + t + 1)
                nc.scalar.activation(q_s[:, t, :], q_w[:, t, :], ACT.Ln, bias=1.0).then_inc(q_s_ready, 1)

            def k_square(sl, b):
                act.wait_ge(k_added, NT * (b + 1))
                if needed(9 * b):
                    act.wait_ge(kv_ready, 9 * b)
                nc.scalar.activation(k_w[:], k_in[:], ACT.Square).then_inc(k_step, 1)

            def k_rnorm(b):
                act.wait_ge(k_rn, 6 * b + 2)
                nc.scalar.activation(kln[:], ksq[:], ACT.Ln, scale=LIFT).then_inc(k_step, 1)
                act.wait_ge(k_step, 4 * b + 2)
                nc.scalar.activation(krn[:], kln[:], ACT.Exp, scale=-0.5, bias=unlift[:]).then_inc(k_step, 1)

            def k_softplus(b):
                act.wait_ge(k_rn, 6 * b + 6)
                act.wait_ge(consts, 1)
                nc.scalar.activation(k_w[:], k_w[:], ACT.Exp).then_inc(k_step, 1)
                act.wait_ge(k_step, 4 * b + 4)
                nc.scalar.activation(k_w[:], k_w[:], ACT.Ln, bias=1.0).then_inc(k_s_ready, 1)

            def reciprocal(sl, images):
                for t in range(CT):
                    it = sl["den", t]
                    act.wait_ge(it.full, it.filled)
                    src = it.tile
                    if needed(ORDERS * CT * (images - 1)):
                        act.wait_ge(out_ready, ORDERS * CT * (images - 1))
                    nc.scalar.activation(x2[:, t, :], src[:], ACT.Ln).then_inc(it.free, 1)
                for t in range(CT):
                    it = sl["den", t]
                    act.wait_ge(it.free, it.filled)
                nc.scalar.activation(x2[:], x2[:], ACT.Exp, scale=-1.0).then_inc(rec_ready, 1)

            def upper_x2(images):
                for t in range(CT):
                    act.wait_ge(x2_ready, CT * (images - 1) + t + 1)
                    nc.scalar.copy(x2_u[:, t, :], x2[:, t, :]).then_inc(x2_u_ready, 1)

            def reorder(sl, images):
                if needed(DMA * (images - 1)):
                    act.wait_ge(out_sent, DMA * (images - 1))
                for m in range(CT):
                    it = sl["mlp", m]
                    act.wait_ge(it.free, it.filled)
                    for image_, windows in orders(res[:, m, :], x2[:, m, :]):
                        nc.scalar.copy(image_, windows).then_inc(out_ready, 1)

            nc.scalar.preload_act_table_set("natural_log_exp_and_others")
            act.wait_ge(w_ready, 1)
            act.wait_ge(consts, 1)
            prepare(0, 0)
            upper_x1(0, 0, None)

            def image(b, p, sl, first=False, last=False):
                for t in range(CT):
                    q_parts(sl, b, t)
                if not last:
                    prepare(b + 1, 1 - p)
                k_square(sl, b)
                for t in range(CT):
                    q_rnorm(b, t)
                k_rnorm(b)
                if not first:
                    reciprocal(sl, b)
                k_softplus(b)
                if not first:
                    it = sl["num", 1]
                    act.wait_ge(it.full, it.filled)
                for t in range(CT):
                    q_softplus(b, t)
                if not last:
                    upper_x1(b + 1, 1 - p, sl)
                if not first:
                    upper_x2(b)
                    reorder(sl, b)

            for_images(act, image)
            reciprocal(tail_slots, B)
            upper_x2(B)
            reorder(tail_slots, B)

        @block.vector
        def _(dve):
            dve.wait_ge(w_in, 8 * DMA)
            nc.vector.tensor_copy(w_u[:], w_f).then_inc(w_split, 1)
            dve.wait_ge(w_split, 1)
            nc.vector.tensor_tensor(w_l[:], w_f, w_u[:].bitcast(F32), ALU.subtract).then_inc(w_split, 1)
            nc.vector.tensor_scalar(centre[:], tap[:, :, 4], 1.0, None, ALU.add).then_inc(w_split, 1)
            dve.wait_ge(mlp_made, 1)
            for m in range(CT):
                nc.vector.tensor_copy(m_u[:, m, :], early[m][:, 0:C]).then_inc(w_split, 1)
            dve.wait_ge(w_split, 5)
            for m in range(CT):
                nc.vector.tensor_tensor(m_l[:, m, :], early[m][:, 0:C], m_u[:, m, :].bitcast(F32),
                                        ALU.subtract).then_inc(w_split, 1)
            nc.vector.tensor_tensor(mlp_bias[:], early[2][:, 0:CT], fc2_b, ALU.add).then_inc(w_split, 1)
            dve.wait_ge(w_split, 8)
            dve.sem_inc(w_ready, 1)

            def convolve(b, taps_):
                around = [(dy, dx) for dy in range(3) for dx in range(3) if (dy, dx) != (1, 1)]
                for n in taps_:
                    dy, dx = around[n]
                    for t in range(CT):
                        if n == 0:
                            dve.wait_ge(centred, CT * b + t + 1)
                        else:
                            dve.wait_ge(tapped[t], 8 * b + n)
                        nc.vector.scalar_tensor_tensor(
                            out=image_view(x1[:, t, :]), in0=y_pad[:, t, dy:dy + SIDE, dx:dx + SIDE],
                            scalar=tap[:, t, 3 * dy + dx:3 * dy + dx + 1], in1=image_view(x1[:, t, :]), op0=ALU.mult,
                            op1=ALU.add).then_inc(tapped[t], 1)

            def add_bias(sl, b, u):
                it = sl["kv", u]
                dve.wait_ge(it.full, it.filled)
                src = it.tile
                tiles = list(enumerate(TILES))[2 * u:2 * u + 2]
                for i, (n, (_, _, tokens)) in enumerate(tiles):
                    at_ = i * HALF
                    nc.vector.tensor_tensor(k_in[0:tokens, n, :], src[0:tokens, at_:at_ + C], kvb[0:tokens, 0:C],
                                            ALU.add).then_inc(k_added, 1)
                    nc.vector.tensor_tensor(
                        v1[0:tokens, n, :, 0:P], src[0:tokens, at_ + C:at_ + 2 * C].rearrange("p (t d) -> p t d", t=CT),
                        kvb[0:tokens, C:].rearrange("p (t d) -> p t d", t=CT), ALU.add).then_inc(
                            it.free if i == len(tiles) - 1 else v_added, 1)

            def split_v(sl, b):
                it = sl["kv", (NT - 1) // 2]
                dve.wait_ge(it.free, it.filled)
                shape = [P, len(CUT), CT * (P + 2)]
                nc.vector.tensor_tensor(
                    v_cut[:].rearrange("p w t d -> p w (t d)"),
                    v1[:, NT - 1, :, :].rearrange("p t d -> p (t d)").unsqueeze(1).broadcast_to(shape),
                    cut_mask[:].unsqueeze(2).broadcast_to(shape), ALU.mult).then_inc(v_split, 1)

            def clamp_q(sl, b, t):
                it = sl["norm", t]
                dve.wait_ge(it.full, it.filled)
                src = it.tile
                nc.vector.tensor_scalar(q_w[:, t, :], src[:], NORM_MIN ** 2, None, ALU.max).then_inc(q_clamped, 1)
                dve.wait_ge(q_clamped, CT * b + t + 1)
                dve.sem_inc(it.free, 1)

            def k_norms(b):
                n = 6 * b
                dve.wait_ge(k_step, 4 * b + 1)
                nc.vector.tensor_reduce(ksq[:], k_w[:].rearrange("p n (h d) -> p (n h) d", d=HD), AX.X,
                                        ALU.add).then_inc(k_rn, 1)
                dve.wait_ge(k_rn, n + 1)
                nc.vector.tensor_scalar(ksq[:], ksq[:], NORM_MIN ** 2, None, ALU.max).then_inc(k_rn, 1)
                dve.wait_ge(k_step, 4 * b + 3)
                nc.vector.tensor_tensor(knw[:], krn[:], ksq[:], ALU.mult).then_inc(k_rn, 1)
                dve.wait_ge(k_rn, n + 3)
                nc.vector.tensor_tensor(knw[:], knw[:], krn[:], ALU.mult).then_inc(k_rn, 1)
                dve.wait_ge(k_rn, n + 4)
                nc.vector.tensor_scalar(knw[:], knw[:], -0.5, 1.5, ALU.mult, ALU.add).then_inc(k_n, 1)
                dve.wait_ge(k_n, 2 * b + 1)
                nc.vector.tensor_tensor(knw[:], knw[:], krn[:], ALU.mult).then_inc(k_n, 1)
                dve.wait_ge(k_n, 2 * b + 2)
                by_head = k_w[:].rearrange("p n (h d) -> p (n h) d", d=HD)
                nc.vector.tensor_tensor(by_head, k_in[:].rearrange("p n (h d) -> p (n h) d", d=HD),
                                        knw[:].unsqueeze(2).broadcast_to([P, NT * HEADS1, HD]), ALU.mult).then_inc(k_rn, 1)
                dve.wait_ge(k_rn, n + 5)
                dve.sem_inc(k_rn, 1)

            def tables(sl, b, u):
                it = sl["state", u]
                dve.wait_ge(it.full, it.filled)
                src = it.tile
                cells = src[:].rearrange("p (a n) -> p a n", a=2)[:, :, 0:3 * (P + 2)].rearrange(
                    "p a (w e) -> p a w e", e=P + 2)
                shape = [P, 2, 3, P]

                def by_cell(tile):
                    return tile[:, 6 * u:6 * u + 6, :].rearrange("p (a w) e -> p a w e", w=3)

                def mask(tile):
                    return tile[:].unsqueeze(1).unsqueeze(1).broadcast_to(shape)

                nc.vector.tensor_tensor(by_cell(kv), cells[:, :, :, 0:P], mask(head_scale), ALU.mult).then_inc(kv_ready, 1)
                for a in range(2):
                    nc.vector.scalar_tensor_tensor(
                        out=by_cell(ks)[:, a], in0=cells[:, a, :, P:P + 1].broadcast_to([P, 3, P]), scalar=EPS,
                        in1=head_ones[:].unsqueeze(1).broadcast_to([P, 3, P]), op0=ALU.add,
                        op1=ALU.mult).then_inc(kv_ready, 1)
                dve.wait_ge(kv_ready, 9 * b + 3 * u + 3)
                dve.sem_inc(it.free, 1)

            def weighted(sl, images):
                dve.wait_ge(rec_ready, images)
                for t in range(CT):
                    it = sl["num", t]
                    dve.wait_ge(it.full, it.filled)
                    src = it.tile
                    nc.vector.tensor_tensor(x2[:, t, :], src[:], x2[:, t, :], ALU.mult).then_inc(it.free, 1)

            def finish(sl, images, m):
                it = sl["mlp", m]
                dve.wait_ge(it.full, it.filled)
                src = it.tile
                nc.vector.scalar_tensor_tensor(out=x2[:, m, :], in0=src[:], scalar=mlp_bias[:, m:m + 1], in1=x2[:, m, :],
                                               op0=ALU.add, op1=ALU.add).then_inc(it.free, 1)

            convolve(0, range(8))

            def image(b, p, sl, first=False, last=False):
                for u in range((NT + 1) // 2):
                    add_bias(sl, b, u)
                split_v(sl, b)
                for t in range(CT):
                    clamp_q(sl, b, t)
                k_norms(b)
                if not first:
                    weighted(sl, b)
                if not last:
                    convolve(b + 1, range(8))
                for u in range(3):
                    tables(sl, b, u)
                if not first:
                    for m in range(CT):
                        finish(sl, b, m)

            for_images(dve, image)
            weighted(tail_slots, B)
            for m in range(CT):
                finish(tail_slots, B, m)

        @block.gpsimd
        def _(pool):
            made = [0]

            def const(instruction):
                made[0] += 1
                instruction.then_inc(c_step, 1)
                pool.wait_ge(c_step, made[0])

            const(nc.gpsimd.memset(y_pad[:], 0.0))
            const(nc.gpsimd.memset(k_in[:], 0.0))
            const(nc.gpsimd.memset(v1[:], 0.0))
            for n, (_, _, tokens) in enumerate(TILES):
                rows = P if n == NT - 1 else tokens
                const(nc.gpsimd.memset(v1[0:rows, n, :, P:P + 1], 1.0))
            const(nc.gpsimd.memset(cut_mask[:], 1.0))
            for base, step, row in ((0, -WS * EDGE, 1), (WS * EDGE - 1, WS * EDGE, -1), (sum(CUT) - 1, 0, -1)):
                const(nc.gpsimd.affine_select(out=cut_mask[:], in_=cut_mask[:], compare_op=ALU.is_ge, fill=0.0, base=base,
                                              pattern=[[step, len(CUT)]], channel_multiplier=row))
            for i, size in enumerate(CUT):
                column = cut_mask[:, i:i + 1]
                const(nc.gpsimd.affine_select(out=column, in_=column, compare_op=ALU.not_equal, fill=float(WS * WS - size),
                                              base=-PAD, pattern=[[0, 1]], channel_multiplier=1))
            pool.sem_inc(v_inited, 1)
            for tile, value in ((head_ones, 1.0), (head_scale, SCALE)):
                const(nc.gpsimd.memset(tile[:], value))
                v = tile[:].rearrange("p (g c) -> p g c", c=HD)
                const(nc.gpsimd.affine_select(out=v, in_=v, compare_op=ALU.is_ge, fill=0.0, base=0,
                                              pattern=[[-HD, P // HD], [0, HD]], channel_multiplier=1))
                const(nc.gpsimd.affine_select(out=v, in_=v, compare_op=ALU.is_ge, fill=0.0, base=HD - 1,
                                              pattern=[[HD, P // HD], [0, HD]], channel_multiplier=-1))
            const(nc.gpsimd.memset(unlift[:], 0.5 * math.log(LIFT)))
            pool.sem_inc(consts, 1)

            def normalise_q(b, t):
                n = CT * b + t
                pool.wait_ge(q_rn, 2 * n + 2)
                nc.gpsimd.tensor_tensor(q_w[:, t, :], q_f[:, t, :], q_w[:, t, :], ALU.mult).then_inc(q_n, 1)

            def add_attention(sl, p, t):
                it = sl["num", t]
                pool.wait_ge(it.free, it.filled)
                nc.gpsimd.tensor_tensor(x2[:, t, :], x1w[p][:, t, :], x2[:, t, :], ALU.add).then_inc(x2_ready, 1)

            def lower_x1(b, p):
                for t in range(CT):
                    pool.wait_ge(x1_u_ready, CT * b + t + 1)
                    nc.gpsimd.tensor_tensor(x1_l[:, t, :], x1w[p][:, t, :], x1_u[:, t, :].bitcast(F32),
                                            ALU.subtract).then_inc(x1_l_ready, 1)

            def lower_x2(images):
                for t in range(CT):
                    pool.wait_ge(x2_u_ready, CT * (images - 1) + t + 1)
                    nc.gpsimd.tensor_tensor(x2_l[:, t, :], x2[:, t, :], x2_u[:, t, :].bitcast(F32),
                                            ALU.subtract).then_inc(x2_l_ready, 1)

            lower_x1(0, 0)

            def image(b, p, sl, first=False, last=False):
                for t in range(CT):
                    normalise_q(b, t)
                if not first:
                    for t in range(CT):
                        add_attention(sl, 1 - p, t)
                if not last:
                    lower_x1(b + 1, 1 - p)
                if not first:
                    lower_x2(b)

            for_images(pool, image)
            for t in range(CT):
                add_attention(tail_slots, (B - 1) % 2, t)
            lower_x2(B)


def program(nc, x, vectors0, qkv_wT, p_wT, vectors1, taps, wqkvT, kv_bias, fc1, fc2T, out):
    y = nc.dram_tensor("layer0_out", x.shape, F32).ap()
    layer0(nc, x, vectors0, qkv_wT, p_wT, y)
    layer1(nc, y, vectors1, taps, wqkvT, kv_bias, fc1, fc2T, out)


def kernel(**inputs):
    import numpy as _np
    import concourse.bacc as _bacc
    from concourse import mybir as _mybir
    from concourse.bass_utils import run_bass_kernel_spmd as _run

    a = {name: _np.asarray(value) for name, value in inputs.items()}
    B, C, H, W = a["x"].shape

    def columns(*names):
        return _np.ascontiguousarray(_np.concatenate([a[n].reshape(-1, P) for n in names]).T)

    wqkv, bqkv = a["L1_conv_wqkv"], a["L1_conv_bqkv"]
    a["q_bias"] = bqkv[:C]
    arrays = {
        "x": _np.ascontiguousarray(a["x"].reshape(B, C, H * W)),
        "vectors0": columns("L0_conv_n_weight", "L0_conv_n_bias", "L0_conv_p_b", "L0_conv_qkv_b"),
        "qkv_wT": _np.ascontiguousarray(a["L0_conv_qkv_w"].T),
        "p_wT": _np.ascontiguousarray(a["L0_conv_p_w"].T),
        "vectors1": columns("L1_conv_conv_b", "q_bias", "L1_conv_bfc2", "L1_conv_bfc1"),
        "taps": _np.ascontiguousarray(a["L1_conv_conv_w"].reshape(C, 9)),
        "wqkvT": _np.ascontiguousarray(wqkv.T),
        "kv_bias": _np.ascontiguousarray(bqkv[C:]),
        "fc1": _np.ascontiguousarray(a["L1_conv_wfc1"]),
        "fc2T": _np.ascontiguousarray(a["L1_conv_wfc2"].T),
    }
    nc = _bacc.Bacc("TRN2", target_bir_lowering=False, num_devices=1)
    args = [nc.dram_tensor(f"in_{name}", v.shape, _mybir.dt.from_np(v.dtype), kind="ExternalInput").ap()
            for name, v in arrays.items()]
    args.append(nc.dram_tensor("out_0", (B, C, H * W), F32, kind="ExternalOutput").ap())
    program(nc, *args)
    r = _run(nc, [{f"in_{name}": v for name, v in arrays.items()}], core_ids=[0])
    return r.results[0]["out_0"].reshape(B, C, H, W)
```

```python
import math
from contextlib import ExitStack

import concourse.bass as bass
from concourse import mybir

P = 128
F32 = mybir.dt.float32
F32R = mybir.dt.float32r
ALU = mybir.AluOpType
ACT = mybir.ActivationFunctionType
AX = mybir.AxisListType

RING = 4
WHOLE_RING = 4
LAG = 2
HALF = 512
DMA = 16
SLOTS = 3


def channel_tiles(ap):
    return ap.rearrange("(t p) n -> p t n", p=P)



HEADS0 = 4
MAX_AT = (2, 2, 2, 3, 3, 4, 4, 5)
TURN_AT = 6
V_AT = ((0, 0), (0, 1))
QK_AT = {1: ((0, 5), (0, 7)), 0: ((2, 6), (2, 7))}
STATS_AT, GROUP_AT, AFFINE_AT = (1, 6), ((2, 0), (2, 1)), (2, 1)
NORM_AT = ((2, 2), (2, 3))
SUM_AT, DIVIDE_AT, OUT_AT = 1, 3, 5
PROJ_AT = {1: ((3, 0), (3, 1)), 0: ((1, 0), (1, 1))}
BEGIN_Y_AT = (1, 3)


def products0(first, last):
    order = []
    for h in range(HEADS0):
        for j in range(8):
            order.append(("scores", h, j))
            if not (last and h == 3):
                order += [("max", (h + 1) % HEADS0, i) for i in range(8) if MAX_AT[i] == j]
                if j == TURN_AT:
                    order.append(("maxT", (h + 1) % HEADS0))
            order += [("v", u) for u in range(2) if V_AT[u] == (h, j)]
            order += [("qk", 1, what) for what in range(2) if QK_AT[1][what] == (h, j)]
            if not last:
                order += [("group", second) for second in (False, True) if GROUP_AT[second] == (h, j)]
                order += [("qk", 0, what) for what in range(2) if QK_AT[0][what] == (h, j)]
            order += [("proj", 1, m) for m in range(2) if PROJ_AT[1][m] == (h, j)]
            if not first:
                order += [("proj", 0, m) for m in range(2) if PROJ_AT[0][m] == (h, j)]
            if j == SUM_AT and not (first and h == 0):
                order.append(("sum", h))
    return order


HEAD_ORDER = ([("group", False), ("group", True), ("qk", 0, 0), ("qk", 0, 1)]
              + [("max", 0, i) for i in range(8)] + [("maxT", 0)])
TAIL_ORDER = [("sum", 0), ("proj", 0, 0), ("proj", 0, 1)]


def needed(count):
    return not isinstance(count, int) or count > 0


class Product:

    def __init__(self, tile, full, free, turn, loops):
        self.tile, self.full, self.free, self.turn, self.loops = tile, full, free, turn, loops

    @property
    def filled(self):
        return self.loops + (self.turn + 1)

    @property
    def emptied(self):
        return self.loops + self.turn


class Slots:

    def __init__(self, slots, order, before, loops=0, per=0):
        assert len(set(order)) == len(order) and per % len(slots) == 0
        self.slots, self.loops = slots, loops * (per // len(slots))
        self.at = {name: before + k for k, name in enumerate(order)}

    def __getitem__(self, name):
        turn, slot = divmod(self.at[name], len(self.slots))
        return Product(*self.slots[slot], turn, self.loops)


def layer0(nc, x, vectors, qkv_wT, p_wT, y):
    B, C, N = x.shape
    CT = C // P
    JT = N // P
    HD = C // HEADS0
    GROUP = C // 8
    VH = HEADS0 * 2 * HD
    SCALE = float(HD) ** -0.5
    EPS = 1e-5
    assert (C, N) == (256, 1024)

    PER = len(products0(False, False))
    BEFORE_FIRST = len(HEAD_ORDER)
    BEFORE_MID = BEFORE_FIRST + len(products0(True, False))
    BEFORE_LAST = BEFORE_MID + (B - 2) * PER
    BEFORE_TAIL = BEFORE_LAST + len(products0(False, True))

    with ExitStack() as ctx:
        def sb(name, shape, dt=F32):
            return ctx.enter_context(nc.sbuf_tensor(name, shape, dt))

        def sem(name):
            return ctx.enter_context(nc.semaphore(name))

        qkv_u, qkv_l = sb("qkv_u", [P, CT, 3 * C], F32R), sb("qkv_l", [P, CT, 3 * C], F32R)
        pw_u, pw_l = sb("pw_u", [P, CT, C], F32R), sb("pw_l", [P, CT, C], F32R)
        vecs = sb("vecs0", [P, 6 * CT])
        gnw, gnb, pb = (vecs[:, i * CT:(i + 1) * CT] for i in range(3))
        qkv_bias = vecs[:, 3 * CT:]
        out_bias = sb("out_bias", [P, CT])
        ident = sb("ident0", [P, P])
        group_mean = sb("group_mean", [P, P])
        ones = sb("ones", [P, P])
        xt = sb("xt", [P, CT, N])
        yt = sb("yt", [P, CT, N])
        xn_u, xn_l = sb("xn_u", [P, CT, N], F32R), sb("xn_l", [P, CT, N], F32R)
        stats, mv = sb("stats", [P, CT, 2, 6]), sb("mv", [P, CT, 2])
        gmean, dev, spread, gvar, lnvar, rstd, newton, gn_a, gn_c = (
            sb(n, [P, CT]) for n in ("gmean", "dev", "spread", "gvar", "lnvar", "rstd", "newton", "gn_a", "gn_c"))
        qk_u, qk_l = sb("qk_u", [P, 2, N], F32R), sb("qk_l", [P, 2, N], F32R)
        key1, key2 = sb("key1", [P, HEADS0, N], F32R), sb("key2", [P, 2, N], F32R)
        qry1, qry2 = sb("qry1", [P, HEADS0, N], F32R), sb("qry2", [P, 2, N], F32R)
        v_ul = sb("v_ul", [P, JT, HEADS0, 2, HD], F32R)
        neg_max = sb("neg_max", [P, JT])
        p_f = sb("p_f", [P, WHOLE_RING, N])
        p_u, p_l = sb("p_u", [P, RING, N], F32R), sb("p_l", [P, RING, N], F32R)
        psums = sb("psums", [P, 2, N])
        rec = sb("rec", [P, N])
        o_f, o_n = sb("o_f", [P, N]), sb("o_n", [P, N])
        o_u, o_l = sb("o_u", [P, N], F32R), sb("o_l", [P, N], F32R)
        xn_f = psums[:, 1, :]
        assert (2, SUM_AT) < NORM_AT[0] < NORM_AT[1] < (3, 0)
        qkv_f = p_f[:].rearrange("p a n -> p (a n)")[:, 0:CT * 3 * C].rearrange("p (t o) -> p t o", t=CT)
        pw_f = psums[:].rearrange("p a n -> p (a n)")[:, 0:CT * C].rearrange("p (t o) -> p t o", t=CT)

        av = ctx.enter_context(nc.psum_tensor("av", [P, 2 * HALF], F32))
        slots = [(ctx.enter_context(nc.psum_tensor(f"slot{i}", [P, 2 * HALF], F32)),
                  sem(f"slot_full{i}"), sem(f"slot_free{i}")) for i in range(SLOTS)]
        head_slots = Slots(slots, HEAD_ORDER, 0)
        tail_slots = Slots(slots, TAIL_ORDER, BEFORE_TAIL)

        (weights_in, consts_made, rows_made, weights_split, bias_made, v_bias_full, x_in, y_begun, y_out, gn_made,
         rstd_ready, xn_u_ready, xn_f_ready, xn_l_ready, qk_u_ready, v_u_ready, p_u_ready, p_l_ready, p_added,
         p_used, av_free, o_low_ready, rec_ready, o_n_ready, o_u_ready, o_l_ready) = (
            sem(n) for n in (
             "weights_in", "consts_made", "rows_made", "weights_split", "bias_made", "v_bias_full", "x_in", "y_begun",
             "y_out", "gn_made", "rstd_ready", "xn_u_ready", "xn_f_ready", "xn_l_ready", "qk_u_ready", "v_u_ready",
             "p_u_ready", "p_l_ready", "p_added", "p_used", "av_free", "o_low_ready",
             "rec_ready", "o_n_ready", "o_u_ready", "o_l_ready"))
        stacked1 = [sem(f"stacked1_{h}") for h in range(HEADS0)]
        stacked2 = [sem(f"stacked2_{h}") for h in range(HEADS0)]
        const_step, shift_made = sem("const_step"), sem("shift_made")
        stats_waited, waited = sem("stats_waited"), sem("waited")
        GN_OPS = 16

        def for_images(eng, image):
            image(0, Slots(slots, products0(True, False), BEFORE_FIRST), first=True)
            with eng.Fori(1, B - 1) as b:
                image(b, Slots(slots, products0(False, False), BEFORE_MID - PER, b, PER))
            image(B - 1, Slots(slots, products0(False, True), BEFORE_LAST), last=True)

        halves = [slice(0, HALF), slice(HALF, 2 * HALF)]
        block = ctx.enter_context(nc.Block())

        @block.sync
        def _(sp):
            sp.dma_start(xt[:], channel_tiles(x[0])).then_inc(x_in, DMA)
            sp.dma_start(vecs[:], vectors).then_inc(weights_in, DMA)
            sp.dma_start(qkv_f, channel_tiles(qkv_wT)).then_inc(weights_in, DMA)
            sp.dma_start(pw_f, channel_tiles(p_wT)).then_inc(weights_in, DMA)

            def stack1(b, h):
                read = 8 * (4 * b + h - 3)
                if needed(read):
                    sp.wait_ge(p_u_ready, read)
                rows, top, low = slice(HD * (h % 2), HD * (h % 2) + HD), slice(0, HD), slice(HD, P)
                for dst, src in ((qry1[top, h, :], qk_u[rows, 0, :]), (key1[top, h, :], qk_u[rows, 1, :]),
                                 (qry1[low, h, :], qk_u[rows, 0, :]), (key1[low, h, :], qk_l[rows, 1, :])):
                    sp.dma_start(dst.bitcast(F32), src.bitcast(F32)).then_inc(stacked1[h], DMA)

            def stack2(b, h):
                if needed(8 * (4 * b + h - 1)):
                    sp.wait_ge(p_u_ready, 8 * (4 * b + h - 1))
                rows, top = slice(HD * (h % 2), HD * (h % 2) + HD), slice(0, HD)
                for dst, src in ((key2[top, h % 2, :], qk_u[rows, 1, :]), (qry2[top, h % 2, :], qk_l[rows, 0, :])):
                    sp.dma_start(dst.bitcast(F32), src.bitcast(F32)).then_inc(stacked2[h], DMA)

            sp.wait_ge(rows_made, 6)
            it = head_slots["qk", 0, 0]
            sp.wait_ge(it.free, it.filled)
            sp.sem_inc(waited, 1)
            it = head_slots["qk", 0, 1]
            sp.wait_ge(it.free, it.filled)
            sp.sem_inc(waited, 1)
            stack1(0, 0)
            stack2(0, 0)
            stack1(0, 1)

            def image(b, sl, first=False, last=False):
                stack2(b, 1)
                it = sl["qk", 1, 0]
                sp.wait_ge(it.free, it.filled)
                sp.sem_inc(waited, 1)
                it = sl["qk", 1, 1]
                sp.wait_ge(it.free, it.filled)
                sp.sem_inc(waited, 1)
                stack1(b, 2)
                stack1(b, 3)
                stack2(b, 2)
                if not first:
                    it = sl["proj", 0, 0]
                    sp.wait_ge(it.free, it.filled)
                    sp.sem_inc(waited, 1)
                    it = sl["proj", 0, 1]
                    sp.wait_ge(it.free, it.filled)
                    sp.sem_inc(waited, 1)
                    sp.dma_start(channel_tiles(y[b - 1]), yt[:]).then_inc(y_out, DMA)
                if not last:
                    coming = channel_tiles(x[b + 1])
                    sp.wait_ge(y_begun, CT * (b + 1))
                    sp.dma_start(xt[:], coming).then_inc(x_in, DMA)
                stack2(b, 3)
                if not last:
                    it = sl["qk", 0, 0]
                    sp.wait_ge(it.free, it.filled)
                    sp.sem_inc(waited, 1)
                    it = sl["qk", 0, 1]
                    sp.wait_ge(it.free, it.filled)
                    sp.sem_inc(waited, 1)
                    stack1(b + 1, 0)
                    stack1(b + 1, 1)
                    stack2(b + 1, 0)

            for_images(sp, image)
            for m in range(CT):
                it = tail_slots["proj", 0, m]
                sp.wait_ge(it.free, it.filled)
            sp.dma_start(channel_tiles(y[B - 1]), yt[:]).then_inc(y_out, DMA)
            sp.wait_ge(y_out, DMA * B)

        @block.tensor
        def _(pe):
            def product(out, left, right):
                terms = [(l, r) for (lu, ll), (ru, rl) in zip(left, right) for l, r in ((lu, ru), (lu, rl), (ll, ru))]
                for n, (l, r) in enumerate(terms):
                    mm = nc.tensor.matmul(out, l, r, start=(n == 0), stop=(n == len(terms) - 1))
                return mm

            def group(sl, images, second):
                pe.wait_ge(gn_made, GN_OPS * (images - 1) + (9 if second else 6))
                to = sl["group", second]
                if needed(to.emptied):
                    pe.wait_ge(to.free, to.emptied)
                out = to.tile
                nc.tensor.matmul(out[:, 0:CT], group_mean[:], spread[:] if second else mv[:, :, 0],
                                 start=True, stop=True).then_inc(to.full, 1)

            def qk(sl, images, pair, what):
                pe.wait_ge(xn_l_ready, CT * images)
                to = sl["qk", pair, what]
                if needed(to.emptied):
                    pe.wait_ge(to.free, to.emptied)
                out = to.tile
                o = what * C + pair * P
                for n in halves:
                    mm = product(out[:, n], [(qkv_u[:, k, o:o + P], qkv_l[:, k, o:o + P]) for k in range(CT)],
                                 [(xn_u[:, k, n], xn_l[:, k, n]) for k in range(CT)])
                mm.then_inc(to.full, 1)

            def values(sl, u):
                to = sl["v", u]
                if needed(to.emptied):
                    pe.wait_ge(to.free, to.emptied)
                out = to.tile
                for i in range(4):
                    j = slice((4 * u + i) * P, (4 * u + i + 1) * P)
                    mm = product(out[:, i * C:(i + 1) * C], [(xn_u[:, k, j], xn_l[:, k, j]) for k in range(CT)],
                                 [(qkv_u[:, k, 2 * C:], qkv_l[:, k, 2 * C:]) for k in range(CT)])
                mm.then_inc(to.full, 1)

            def row_scores(sl, b, h, i):
                if i == 0:
                    pe.wait_ge(stacked1[h % HEADS0], 4 * DMA * (b + h // HEADS0 + 1))
                to = sl["max", h % HEADS0, i]
                if needed(to.emptied):
                    pe.wait_ge(to.free, to.emptied)
                out = to.tile
                for n in halves:
                    mm = nc.tensor.matmul(out[:, n], qry1[:, h % HEADS0, i * P:(i + 1) * P], key1[:, h % HEADS0, n],
                                          start=True, stop=True)
                mm.then_inc(to.full, 1)

            def turn_max(sl, h):
                for i in range(5, 8):
                    it = sl["max", h, i]
                    pe.wait_ge(it.free, it.filled)
                to = sl["maxT", h]
                if needed(to.emptied):
                    pe.wait_ge(to.free, to.emptied)
                out = to.tile
                nc.tensor.transpose(out[0:JT, 0:P], neg_max[:], ident[:]).then_inc(to.full, 1)

            def scores(sl, b, h, j):
                s, jj = h % 2, slice(j * P, (j + 1) * P)
                if j == 0:
                    pe.wait_ge(stacked2[h], 2 * DMA * (b + 1))
                to = sl["scores", h, j]
                if needed(to.emptied):
                    pe.wait_ge(to.free, to.emptied)
                out = to.tile
                for n in halves:
                    nc.tensor.matmul(out[:, n], key1[:, h, jj], qry1[:, h, n], start=True, stop=False)
                for n in halves:
                    mm = nc.tensor.matmul(out[:, n], key2[:, s, jj], qry2[:, s, n], start=False, stop=True)
                mm.then_inc(to.full, 1)

            def weigh(b, h, j, g):
                if j == 0:
                    if needed(4 * b + h):
                        pe.wait_ge(av_free, 4 * b + h)
                pe.wait_ge(p_l_ready, 32 * b + 8 * h + j + 1)
                r = g % RING
                for n in halves:
                    nc.tensor.matmul(av[:, n], v_ul[:, j, h, :, :].rearrange("p a d -> p (a d)"), p_u[:, r, n],
                                     start=(j == 0), stop=False, skip_group_check=True)
                for n in halves:
                    mm = nc.tensor.matmul(av[0:HD, n], v_ul[:, j, h, 0, :], p_l[:, r, n],
                                          start=False, stop=(j == JT - 1), skip_group_check=True)
                mm.then_inc(p_used, 1)

            def prob_sums(sl, heads, h):
                pe.wait_ge(p_added, 7 * heads)
                to = sl["sum", h]
                if needed(to.emptied):
                    pe.wait_ge(to.free, to.emptied)
                for n in halves:
                    mm = nc.tensor.matmul(to.tile[:, n], ones[:], psums[:, (h - 1) % 2, n], start=True, stop=True)
                mm.then_inc(to.full, 1)

            def project(sl, pairs, pair, at, m):
                pe.wait_ge(o_l_ready, pairs)
                to = sl["proj", at, m]
                if needed(to.emptied):
                    pe.wait_ge(to.free, to.emptied)
                out = to.tile
                mm_ = slice(m * P, (m + 1) * P)
                for n in halves:
                    mm = product(out[:, n], [(pw_u[:, pair, mm_], pw_l[:, pair, mm_])], [(o_u[:, n], o_l[:, n])])
                mm.then_inc(to.full, 1)

            pe.wait_ge(weights_in, 3 * DMA)
            for m in range(CT):
                for k in range(CT):
                    mm = nc.tensor.matmul(av[:, m:m + 1], pw_f[:, k, m * P:(m + 1) * P],
                                          qkv_bias[:, 2 * CT + k:2 * CT + k + 1], start=(k == 0), stop=(k == CT - 1))
            mm.then_inc(v_bias_full, 1)
            pe.wait_ge(consts_made, 1)
            group(head_slots, 1, False)
            group(head_slots, 1, True)
            pe.wait_ge(weights_split, 4)
            qk(head_slots, 1, 0, 0)
            qk(head_slots, 1, 0, 1)
            for i in range(JT):
                row_scores(head_slots, 0, 0, i)
            turn_max(head_slots, 0)
            it = head_slots["maxT", 0]
            pe.wait_ge(it.free, it.filled)
            pe.wait_ge(bias_made, 1)

            def image(b, sl, first=False, last=False):
                for h in range(HEADS0):
                    for j in range(JT):
                        scores(sl, b, h, j)
                        if not (last and h == 3):
                            for i in range(JT):
                                if MAX_AT[i] == j:
                                    row_scores(sl, b, h + 1, i)
                            if j == TURN_AT:
                                turn_max(sl, (h + 1) % HEADS0)
                        for u in range(2):
                            if V_AT[u] == (h, j):
                                values(sl, u)
                        if j >= LAG:
                            if h == 0 and j == LAG:
                                it = sl["v", 0]
                                pe.wait_ge(it.free, it.filled)
                                it = sl["v", 1]
                                pe.wait_ge(it.free, it.filled)
                            weigh(b, h, j - LAG, 8 * h + j - LAG)
                        elif not (first and h == 0):
                            weigh_before(b, h, j)
                        for what in range(2):
                            if QK_AT[1][what] == (h, j):
                                qk(sl, b + 1, 1, what)
                        if not last:
                            for second in (False, True):
                                if GROUP_AT[second] == (h, j):
                                    group(sl, b + 2, second)
                            for what in range(2):
                                if QK_AT[0][what] == (h, j):
                                    qk(sl, b + 2, 0, what)
                        for m in range(CT):
                            if PROJ_AT[1][m] == (h, j):
                                project(sl, 2 * b + 1, 0, 1, m)
                        for m in range(CT):
                            if PROJ_AT[0][m] == (h, j) and not first:
                                project(sl, 2 * b, 1, 0, m)
                        if j == SUM_AT and not (first and h == 0):
                            prob_sums(sl, 4 * b + h, h)
                        if j == 7 and not (last and h == 3):
                            it = sl["maxT", (h + 1) % HEADS0]
                            pe.wait_ge(it.free, it.filled)

            def weigh_before(b, h, j):
                jj = JT - LAG + j
                if h == 0:
                    weigh(b - 1, HEADS0 - 1, jj, 8 * (HEADS0 - 1) + jj)
                else:
                    weigh(b, h - 1, jj, 8 * (h - 1) + jj)

            for_images(pe, image)
            for j in range(LAG):
                weigh(B - 1, HEADS0 - 1, JT - LAG + j, 8 * (HEADS0 - 1) + JT - LAG + j)
            prob_sums(tail_slots, 4 * B, 0)
            project(tail_slots, 2 * B, 1, 0, 0)
            project(tail_slots, 2 * B, 1, 0, 1)

        @block.scalar
        def _(act):
            def copy_qk(sl, pairs, pair, what):
                for h in (0, 1) if pair else (2, 3):
                    if needed(pairs - 1):
                        n = (pairs - 1 + pair) // 2
                        act.wait_ge(stacked1[h], 4 * DMA * n)
                        act.wait_ge(stacked2[h], 2 * DMA * n)
                it = sl["qk", pair, what]
                act.wait_ge(it.full, it.filled)
                src = it.tile
                nc.scalar.activation(qk_u[:, what, :], src[:], ACT.Identity,
                                     bias=qkv_bias[:, CT * what + pair:CT * what + pair + 1]).then_inc(qk_u_ready, 1)

            def copy_v(sl, b, u):
                if needed(32 * b - 4 + 4 * u):
                    act.wait_ge(p_used, 32 * b - 4 + 4 * u)
                it = sl["v", u]
                act.wait_ge(it.full, it.filled)
                src = it.tile
                nc.scalar.copy(v_ul[:, 4 * u:4 * u + 4, :, 0, :],
                               src[:].rearrange("p (j h d) -> p j h d", j=4, h=HEADS0)).then_inc(v_u_ready, 1)

            def probs(b, sl, h, j):
                g = 8 * h + j
                it = sl["scores", h, j]
                act.wait_ge(it.full, it.filled)
                src = it.tile
                old = 32 * b + g - WHOLE_RING + 1
                if needed(old):
                    act.wait_ge(p_l_ready, old)
                added = 7 * (4 * b + h) + (max(j - WHOLE_RING, 1) if j >= WHOLE_RING else 1 + j - WHOLE_RING)
                if needed(added):
                    act.wait_ge(p_added, added)
                nc.scalar.activation(p_f[:, g % WHOLE_RING, :], src[:], ACT.Exp, scale=SCALE).then_inc(it.free, 1)
                it = sl["scores", h, j]
                act.wait_ge(it.free, it.filled)
                if needed(32 * b + g - RING + 1):
                    act.wait_ge(p_used, 32 * b + g - RING + 1)
                nc.scalar.copy(p_u[:, g % RING, :], p_f[:, g % WHOLE_RING, :]).then_inc(p_u_ready, 1)

            def lower_half(heads, h):
                act.wait_ge(p_used, 8 * heads)
                if needed(heads - 2):
                    act.wait_ge(o_n_ready, heads - 2)
                nc.scalar.copy(o_f[HD * (h % 2):HD * (h % 2) + HD, :], av[HD:P, :]).then_inc(o_low_ready, 1)

            def reciprocal_sums(sl, heads, h):
                it = sl["sum", h]
                act.wait_ge(it.full, it.filled)
                src = it.tile
                if needed(heads - 1):
                    act.wait_ge(o_n_ready, heads - 1)
                nc.scalar.activation(rec[:], src[:], ACT.Ln).then_inc(it.free, 1)
                it = sl["sum", h]
                act.wait_ge(it.free, it.filled)
                nc.scalar.activation(rec[:], rec[:], ACT.Exp, scale=-1.0).then_inc(rec_ready, 1)

            def rough_rstd(images):
                act.wait_ge(gn_made, GN_OPS * (images - 1) + 10)
                nc.scalar.activation(lnvar[:], gvar[:], ACT.Ln).then_inc(rstd_ready, 1)
                act.wait_ge(rstd_ready, 2 * images - 1)
                nc.scalar.activation(rstd[:], lnvar[:], ACT.Exp, scale=-0.5).then_inc(rstd_ready, 1)

            def normalise(images, t):
                act.wait_ge(gn_made, GN_OPS * images)
                for out, s in ((xn_u[:, t, :], xn_u_ready), (xn_f, xn_f_ready)):
                    if s is xn_f_ready and needed(CT * (images - 1) + t):
                        act.wait_ge(xn_l_ready, CT * (images - 1) + t)
                    nc.scalar.activation(out, xt[:, t, :], ACT.Identity, scale=gn_a[:, t:t + 1],
                                         bias=gn_c[:, t:t + 1]).then_inc(s, 1)

            def begin_y(b):
                if needed(DMA * b):
                    act.wait_ge(y_out, DMA * b)
                act.wait_ge(bias_made, 1)
                for t in range(CT):
                    nc.scalar.activation(yt[:, t, :], xt[:, t, :], ACT.Identity,
                                         bias=out_bias[:, t:t + 1]).then_inc(y_begun, 1)

            nc.scalar.preload_act_table_set("natural_log_exp_and_others")
            act.wait_ge(consts_made, 1)
            for s in range(2):
                nc.scalar.copy(qry2[HD:P, s, :], o_n[HD:P, :]).then_inc(rows_made, 1)
                nc.scalar.copy(key2[HD:P, s, :], o_n[HD:P, :]).then_inc(rows_made, 1)
                act.wait_ge(rows_made, 3 * s + 2)
                nc.scalar.copy(key2[HD:HD + JT, s, :], rec[HD:HD + JT, :]).then_inc(rows_made, 1)
            act.wait_ge(weights_in, 3 * DMA)
            rough_rstd(1)
            act.wait_ge(x_in, DMA)
            normalise(1, 0)
            normalise(1, 1)
            copy_qk(head_slots, 1, 0, 0)
            copy_qk(head_slots, 1, 0, 1)
            act.wait_ge(weights_split, 4)

            def image(b, sl, first=False, last=False):
                for h in range(HEADS0):
                    for j in range(JT):
                        probs(b, sl, h, j)
                        for u in range(2):
                            if V_AT[u] == (h, j):
                                copy_v(sl, b, u)
                        if j == LAG - 1 and not (first and h == 0):
                            lower_half(4 * b + h, (h - 1) % HEADS0)
                        for what in range(2):
                            if QK_AT[1][what] == (h, j):
                                copy_qk(sl, 2 * b + 2, 1, what)
                        if (h, j) == BEGIN_Y_AT:
                            begin_y(b)
                        if not last:
                            if (h, j) == GROUP_AT[1]:
                                rough_rstd(b + 2)
                            for t in range(CT):
                                if (h, j) == NORM_AT[t]:
                                    if t == 0:
                                        it = sl["qk", 1, 1]
                                        act.wait_ge(it.free, it.filled)
                                    normalise(b + 2, t)
                            for what in range(2):
                                if QK_AT[0][what] == (h, j):
                                    copy_qk(sl, 2 * b + 3, 0, what)
                        if j == SUM_AT and not (first and h == 0):
                            reciprocal_sums(sl, 4 * b + h, h)

            for_images(act, image)
            lower_half(4 * B, HEADS0 - 1)
            reciprocal_sums(tail_slots, 4 * B, 0)

        @block.vector
        def _(dve):
            def lower_qk(sl, pairs, pair, what):
                dve.wait_ge(qk_u_ready, 2 * (pairs - 1) + what + 1)
                it = sl["qk", pair, what]
                dve.wait_ge(it.full, it.filled)
                src = it.tile
                nc.vector.scalar_tensor_tensor(
                    out=qk_l[:, what, :], in0=src[:], scalar=qkv_bias[:, CT * what + pair:CT * what + pair + 1],
                    in1=qk_u[:, what, :].bitcast(F32), op0=ALU.add, op1=ALU.subtract).then_inc(it.free, 1)

            def lower_v(sl, b, u):
                dve.wait_ge(v_u_ready, 2 * b + u + 1)
                it = sl["v", u]
                dve.wait_ge(it.full, it.filled)
                src = it.tile
                nc.vector.tensor_tensor(
                    v_ul[:, 4 * u:4 * u + 4, :, 1, :], src[:].rearrange("p (j h d) -> p j h d", j=4, h=HEADS0),
                    v_ul[:, 4 * u:4 * u + 4, :, 0, :].bitcast(F32), ALU.subtract).then_inc(it.free, 1)

            def lower_probs(b, sl, h, j):
                g = 8 * h + j
                dve.wait_ge(p_u_ready, 32 * b + g + 1)
                nc.vector.tensor_tensor(p_l[:, g % RING, :], p_f[:, g % WHOLE_RING, :], p_u[:, g % RING, :].bitcast(F32),
                                        ALU.subtract).then_inc(p_l_ready, 1)

            def row_max(sl, h, i):
                it = sl["max", h, i]
                dve.wait_ge(it.full, it.filled)
                src = it.tile
                nc.vector.tensor_reduce(neg_max[:, i:i + 1], src[:], AX.X, ALU.max, negate=True).then_inc(it.free, 1)

            def place_max(sl, h):
                it = sl["maxT", h]
                dve.wait_ge(it.full, it.filled)
                src = it.tile
                nc.vector.tensor_tensor(
                    qry2[HD:HD + JT, h % 2, :].rearrange("p (c n) -> p c n", c=JT),
                    src[0:JT, 0:P].unsqueeze(1).broadcast_to([JT, JT, P]),
                    ident[0:JT, 0:JT].unsqueeze(2).broadcast_to([JT, JT, P]), ALU.mult).then_inc(it.free, 1)

            def join_halves(heads, h):
                dve.wait_ge(o_low_ready, heads)
                rows = slice(HD * (h % 2), HD * (h % 2) + HD)
                nc.vector.tensor_tensor(o_f[rows, :], av[0:HD, :], o_f[rows, :], ALU.add).then_inc(av_free, 1)

            def upper_out(pairs):
                dve.wait_ge(o_n_ready, 2 * pairs)
                nc.vector.tensor_copy(o_u[:], o_n[:]).then_inc(o_u_ready, 1)

            def add_projection(sl, at, m, begun):
                dve.wait_ge(y_begun, begun)
                it = sl["proj", at, m]
                dve.wait_ge(it.full, it.filled)
                src = it.tile
                nc.vector.tensor_tensor(yt[:, m, :], src[:], yt[:, m, :], ALU.add).then_inc(it.free, 1)

            def gn(instruction):
                instruction.then_inc(gn_made, 1)

            def image_stats(images):
                n = GN_OPS * (images - 1)
                dve.wait_ge(x_in, DMA * images)
                for t in range(CT):
                    for half in range(2):
                        gn(nc.vector.bn_stats(stats[:, t, half, :], xt[:, t, halves[half]]))
                dve.wait_ge(gn_made, n + 4)
                dve.sem_inc(stats_waited, 1)
                for t in range(CT):
                    gn(nc.vector.bn_aggr(mv[:, t, :], stats[:, t, :, :]))

            def group_spread(sl, images):
                n = GN_OPS * (images - 1)
                it = sl["group", False]
                dve.wait_ge(it.full, it.filled)
                src = it.tile
                nc.vector.tensor_copy(gmean[:], src[:, 0:CT]).then_inc(it.free, 1)
                it = sl["group", False]
                dve.wait_ge(it.free, it.filled)
                gn(nc.vector.tensor_tensor(dev[:], mv[:, :, 0], gmean[:], ALU.subtract))
                dve.wait_ge(gn_made, n + 7)
                gn(nc.vector.tensor_tensor(newton[:], dev[:], dev[:], ALU.mult))
                dve.wait_ge(gn_made, n + 8)
                gn(nc.vector.tensor_tensor(spread[:], newton[:], mv[:, :, 1], ALU.add))

            def group_var(sl, images):
                it = sl["group", True]
                dve.wait_ge(it.full, it.filled)
                src = it.tile
                gn(nc.vector.tensor_scalar(gvar[:], src[:, 0:CT], EPS, None, ALU.add))
                dve.wait_ge(gn_made, GN_OPS * (images - 1) + 10)
                dve.sem_inc(it.free, 1)

            def group_affine(images):
                n = GN_OPS * (images - 1)
                dve.wait_ge(rstd_ready, 2 * images)
                gn(nc.vector.tensor_tensor(newton[:], rstd[:], rstd[:], ALU.mult))
                dve.wait_ge(gn_made, n + 11)
                gn(nc.vector.tensor_tensor(dev[:], newton[:], gvar[:], ALU.mult))
                dve.wait_ge(gn_made, n + 12)
                gn(nc.vector.tensor_scalar(newton[:], dev[:], -0.5, 1.5, ALU.mult, ALU.add))
                dve.wait_ge(gn_made, n + 13)
                gn(nc.vector.tensor_tensor(dev[:], newton[:], rstd[:], ALU.mult))
                dve.wait_ge(gn_made, n + 14)
                gn(nc.vector.tensor_tensor(gn_a[:], dev[:], gnw, ALU.mult))
                dve.wait_ge(gn_made, n + 15)
                nc.vector.tensor_tensor(newton[:], gmean[:], gn_a[:], ALU.mult).then_inc(shift_made, 1)
                dve.wait_ge(shift_made, images)
                gn(nc.vector.tensor_tensor(gn_c[:], gnb, newton[:], ALU.subtract))

            dve.wait_ge(weights_in, 3 * DMA)
            nc.vector.tensor_copy(qkv_u[:], qkv_f).then_inc(weights_split, 1)
            nc.vector.tensor_copy(pw_u[:], pw_f).then_inc(weights_split, 1)
            dve.wait_ge(weights_split, 2)
            nc.vector.tensor_tensor(qkv_l[:], qkv_f, qkv_u[:].bitcast(F32), ALU.subtract).then_inc(weights_split, 1)
            nc.vector.tensor_tensor(pw_l[:], pw_f, pw_u[:].bitcast(F32), ALU.subtract).then_inc(weights_split, 1)
            dve.wait_ge(v_bias_full, 1)
            nc.vector.tensor_tensor(out_bias[:], av[:, 0:CT], pb, ALU.add).then_inc(bias_made, 1)
            image_stats(1)
            group_spread(head_slots, 1)
            group_var(head_slots, 1)
            group_affine(1)
            lower_qk(head_slots, 1, 0, 0)
            lower_qk(head_slots, 1, 0, 1)
            for i in range(JT):
                row_max(head_slots, 0, i)
            dve.wait_ge(consts_made, 1)
            dve.wait_ge(rows_made, 6)
            place_max(head_slots, 0)

            def image(b, sl, first=False, last=False):
                for h in range(HEADS0):
                    for j in range(JT):
                        if j == LAG and not (first and h == 0):
                            join_halves(4 * b + h, (h - 1) % HEADS0)
                        if not (last and h == 3):
                            for i in range(JT):
                                if MAX_AT[i] == j:
                                    row_max(sl, (h + 1) % HEADS0, i)
                            if j == TURN_AT:
                                place_max(sl, (h + 1) % HEADS0)
                        lower_probs(b, sl, h, j)
                        for u in range(2):
                            if V_AT[u] == (h, j):
                                lower_v(sl, b, u)
                        for what in range(2):
                            if QK_AT[1][what] == (h, j):
                                lower_qk(sl, 2 * b + 2, 1, what)
                        if not last:
                            if (h, j) == STATS_AT:
                                image_stats(b + 2)
                            if (h, j) == GROUP_AT[0]:
                                group_spread(sl, b + 2)
                            if (h, j) == GROUP_AT[1]:
                                group_var(sl, b + 2)
                            if (h, j) == AFFINE_AT:
                                group_affine(b + 2)
                            for what in range(2):
                                if QK_AT[0][what] == (h, j):
                                    lower_qk(sl, 2 * b + 3, 0, what)
                        for m in range(CT):
                            if PROJ_AT[1][m] == (h, j):
                                add_projection(sl, 1, m, CT * (b + 1))
                        for m in range(CT):
                            if PROJ_AT[0][m] == (h, j) and not first:
                                add_projection(sl, 0, m, CT * b)
                        if j == OUT_AT and h % 2 == 0 and not (first and h == 0):
                            upper_out(2 * b + h // 2)

            for_images(dve, image)
            join_halves(4 * B, HEADS0 - 1)
            upper_out(2 * B)
            add_projection(tail_slots, 0, 0, CT * B)
            add_projection(tail_slots, 0, 1, CT * B)

        @block.gpsimd
        def _(pool):
            def add_probs(b, sl, h, j):
                n = 7 * (4 * b + h) + j - 1
                if j == 1:
                    if needed(4 * b + h - 1):
                        pool.wait_ge(rec_ready, 4 * b + h - 1)
                else:
                    pool.wait_ge(p_added, n)
                it = sl["scores", h, j]
                pool.wait_ge(it.free, it.filled)
                acc = psums[:, h % 2, :]
                g = 8 * h + j
                nc.gpsimd.tensor_tensor(acc, p_f[:, (g - 1) % WHOLE_RING, :] if j == 1 else acc, p_f[:, g % WHOLE_RING, :],
                                        ALU.add).then_inc(p_added, 1)

            def divide(heads, h, added):
                rows = slice(HD * (h % 2), HD * (h % 2) + HD)
                pool.wait_ge(p_added, added)
                pool.wait_ge(av_free, heads)
                pool.wait_ge(rec_ready, heads)
                if h % 2 == 0:
                    if needed((heads - 1) // 2):
                        pool.wait_ge(o_l_ready, (heads - 1) // 2)
                nc.gpsimd.tensor_tensor(o_n[rows, :], o_f[rows, :], rec[rows, :], ALU.mult).then_inc(o_n_ready, 1)
                pool.wait_ge(o_n_ready, heads)

            def lower_out(pairs):
                pool.wait_ge(o_u_ready, pairs)
                nc.gpsimd.tensor_tensor(o_l[:], o_n[:], o_u[:].bitcast(F32), ALU.subtract).then_inc(o_l_ready, 1)

            def lower_normed(images, t):
                n = CT * (images - 1) + t
                pool.wait_ge(xn_f_ready, n + 1)
                nc.gpsimd.tensor_tensor(xn_l[:, t, :], xn_f, xn_u[:, t, :].bitcast(F32),
                                        ALU.subtract).then_inc(xn_l_ready, 1)

            made = [0]

            def const(instruction):
                made[0] += 1
                instruction.then_inc(const_step, 1)
                pool.wait_ge(const_step, made[0])

            const(nc.gpsimd.memset(ident[:], 0.0))
            const(nc.gpsimd.affine_select(out=ident[:], in_=ident[:], compare_op=ALU.not_equal, fill=1.0, base=0,
                                          pattern=[[-1, P]], channel_multiplier=1))
            const(nc.gpsimd.memset(group_mean[:], 1.0 / GROUP))
            gm = group_mean[:].rearrange("p (g c) -> p g c", c=GROUP)
            const(nc.gpsimd.affine_select(out=gm, in_=gm, compare_op=ALU.is_ge, fill=0.0, base=0,
                                          pattern=[[-GROUP, P // GROUP], [0, GROUP]], channel_multiplier=1))
            const(nc.gpsimd.affine_select(out=gm, in_=gm, compare_op=ALU.is_ge, fill=0.0, base=GROUP - 1,
                                          pattern=[[GROUP, P // GROUP], [0, GROUP]], channel_multiplier=-1))
            const(nc.gpsimd.memset(ones[:], 1.0))
            const(nc.gpsimd.memset(rec[:], 1.0))
            const(nc.gpsimd.memset(o_n[:], 0.0))
            pool.sem_inc(consts_made, 1)
            lower_normed(1, 0)
            lower_normed(1, 1)
            pool.wait_ge(bias_made, 1)

            def image(b, sl, first=False, last=False):
                for h in range(HEADS0):
                    for j in range(JT):
                        if j:
                            add_probs(b, sl, h, j)
                        if not (first and h == 0):
                            if j == DIVIDE_AT:
                                divide(4 * b + h, (h - 1) % HEADS0, 7 * (4 * b + h) + j)
                            if j == OUT_AT and h % 2 == 0:
                                lower_out(2 * b + h // 2)
                        for t in range(CT):
                            if NORM_AT[t] == (h, j) and not last:
                                lower_normed(b + 2, t)

            for_images(pool, image)
            divide(4 * B, HEADS0 - 1, 7 * 4 * B)
            lower_out(2 * B)



HEADS1 = 8
WS = 15
SIDE = 32
FULL = 2 * WS
EDGE = SIDE - FULL
WHOLE, CUT = 4, [WS * EDGE] * 4 + [EDGE * EDGE]
WINDOWS = [(w * WS * WS, WS * WS) for w in range(WHOLE)]
for size in CUT:
    WINDOWS.append((sum(WINDOWS[-1]), size))
EDGES = WINDOWS[WHOLE][0]
TILES = [(w, WINDOWS[w][0] + i * 113, 113 - i) for w in range(WHOLE) for i in range(2)] + [(None, EDGES, sum(CUT))]
SLOTS1 = 4


def orders(image, windows):
    image = image.rearrange("p (r c) -> p r c", c=SIDE)
    for band in range(2):
        yield (image[:, band * WS:(band + 1) * WS, 0:FULL].rearrange("p r (w c) -> p w r c", c=WS),
               windows[:, band * 2 * WS * WS:(band + 1) * 2 * WS * WS].rearrange("p (w r c) -> p w r c", w=2, c=WS))
    right = windows[:, EDGES:EDGES + FULL * EDGE]
    yield image[:, 0:FULL, FULL:SIDE], right.rearrange("p (r c) -> p r c", c=EDGE)
    low = windows[:, EDGES + FULL * EDGE:EDGES + 2 * FULL * EDGE]
    yield (image[:, FULL:SIDE, 0:FULL].rearrange("p r (w c) -> p w r c", c=WS),
           low.rearrange("p (w r c) -> p w r c", w=2, c=WS))
    yield (image[:, FULL:SIDE, FULL:SIDE],
           windows[:, EDGES + 2 * FULL * EDGE:].rearrange("p (r c) -> p r c", c=EDGE))


ORDERS = 5


PRODUCTS1 = [("kv", 0), ("kv", 1), ("q", 0), ("kv", 2), ("kv", 3), ("q", 1), ("kv", 4), ("norm", 0),
             ("den", 0), ("norm", 1), ("den", 1), ("num", 0), ("num", 1), ("state", 0), ("state", 1),
             ("mlp", 0), ("mlp", 1), ("state", 2)]
OF_LAST = ("den", "num", "mlp")


def products1(first):
    return [(what, i) for what, i in PRODUCTS1 if not (first and what in OF_LAST)]


def layer1(nc, y, vectors, taps, wqkvT, kv_bias, fc1, fc2T, out):
    B, C, N = y.shape
    CT = C // P
    NW = len(WINDOWS)
    NT = len(TILES)
    HD = C // HEADS1
    F = fc1.shape[0]
    FT = F // P
    SCALE = float(HD) ** -0.5
    EPS = 1e-6
    NORM_MIN = 1e-12
    LIFT = 2.0 ** 20
    PAD = P - 1
    assert (C, N, SIDE * SIDE) == (256, 1024, 1024)

    U = len(products1(False))
    U0 = len(products1(True))
    assert 2 * U % SLOTS1 == 0

    with ExitStack() as ctx:
        def sb(name, shape, dt=F32):
            return ctx.enter_context(nc.sbuf_tensor(name, shape, dt))

        def sem(name):
            return ctx.enter_context(nc.semaphore(name))

        w_u, w_l = sb("w_u", [P, CT, 3 * C], F32R), sb("w_l", [P, CT, 3 * C], F32R)
        m_u, m_l = sb("m_u", [P, CT, C], F32R), sb("m_l", [P, CT, C], F32R)
        vecs = sb("vecs1", [P, 3 * CT + FT])
        conv_b, q_bias, fc2_b = (vecs[:, i * CT:(i + 1) * CT] for i in range(3))
        fc1_b = vecs[:, 3 * CT:]
        tap = sb("tap", [P, CT, 9])
        centre = sb("centre", [P, CT])
        mlp_bias = sb("mlp_bias", [P, CT])
        kvb = sb("kvb", [P, 2 * C])
        head_ones = sb("head_ones", [P, P])
        head_scale = sb("head_scale", [P, P])
        unlift, tiny = sb("unlift", [P, 1]), sb("tiny", [P, 1])

        cut_mask = sb("cut_mask", [P, len(CUT)])

        y_in = sb("y_in", [P, CT, N])
        y_pad = sb("y_pad", [P, CT, SIDE + 2, SIDE + 2])
        x1 = sb("x1", [P, CT, N])
        x1w = [sb("x1wa", [P, CT, N]), sb("x1wb", [P, CT, N])]
        x1_u, x1_l = sb("x1_u", [P, CT, N], F32R), sb("x1_l", [P, CT, N], F32R)
        q_f = sb("q_f", [P, CT, N])
        q_w = sb("q_w", [P, CT, N])
        q_s = sb("q_s", [P, CT, N])
        k_in = sb("k_in", [P, NT, C])
        k_w = sb("k_w", [P, NT, C])
        v1 = sb("v1", [P, NT, CT, P + 2])
        v_cut = sb("v_cut", [P, len(CUT), CT, P + 2])
        ksq, kln, krn, knw = (sb(n, [P, NT * HEADS1]) for n in ("ksq", "kln", "krn", "knw"))
        kv, ks = sb("kv", [P, CT * NW, P]), sb("ks", [P, CT * NW, P])
        x2 = sb("x2", [P, CT, N])
        res = sb("res", [P, CT, N])
        x2_u, x2_l = sb("x2_u", [P, CT, N], F32R), sb("x2_l", [P, CT, N], F32R)

        def flat(tile, width):
            return tile[:].rearrange("p a n -> p (a n)")[:, 0:width]

        w_f = flat(q_f, CT * 3 * C).rearrange("p (t o) -> p t o", t=CT)
        fc1_f = flat(x2, FT * C).rearrange("p (t o) -> p t o", t=FT)
        fc2_f = flat(res, FT * C).rearrange("p (t o) -> p t o", t=FT)

        slots = [(ctx.enter_context(nc.psum_tensor(f"slot1_{i}", [P, 2 * HALF], F32)),
                  sem(f"slot1_full{i}"), sem(f"slot1_free{i}")) for i in range(SLOTS1)]
        early = [tile for tile, _, _ in slots]
        tail_slots = Slots(slots, [name for name in PRODUCTS1 if name[0] in OF_LAST], U0 + (B - 1) * U)
        (vectors_in, centre_made, framed, w_in, c_step, consts, w_split, mlp_made, w_ready, y_loaded, padded,
         centred, x1_u_ready, x1_l_ready, q_f_ready, q_ln, q_clamped, q_rn, q_n, q_exp, q_s_ready, k_added,
         k_step, k_rn, k_n, k_s_ready, rec_ready, ordered, v_added, v_split, x2_ready, x2_u_ready, x2_l_ready,
         out_ready, out_sent, kv_ready, v_inited) = (
            sem("l1_" + n) for n in (
                "vectors_in", "centre_made", "framed", "w_in", "c_step", "consts", "w_split", "mlp_made",
                "w_ready", "y_loaded", "padded", "centred", "x1_u_ready", "x1_l_ready", "q_f_ready", "q_ln",
                "q_clamped", "q_rn", "q_n", "q_exp", "q_s_ready", "k_added", "k_step", "k_rn", "k_n",
                "k_s_ready", "rec_ready", "ordered", "v_added", "v_split", "x2_ready", "x2_u_ready",
                "x2_l_ready", "out_ready", "out_sent", "kv_ready", "v_inited"))
        waited = sem("l1_waited")
        tapped = [sem("l1_tapped0"), sem("l1_tapped1")]

        def for_images(eng, image):
            image(0, 0, Slots(slots, products1(True), 0), first=True)
            image(1, 1, Slots(slots, products1(False), U0))
            with eng.Fori(1, B // 2 - 1) as i:
                for p in range(2):
                    image(i * 2 + p, p, Slots(slots, products1(False), U0 + U + p * U - 2 * U, i, 2 * U))
            before = U0 + U + (B // 2 - 2) * 2 * U
            image(B - 2, 0, Slots(slots, products1(False), before))
            image(B - 1, 1, Slots(slots, products1(False), before + U), last=True)

        halves = [slice(0, HALF), slice(HALF, 2 * HALF)]

        def image_view(ap):
            return ap.rearrange("p (r c) -> p r c", c=SIDE)

        block = ctx.enter_context(nc.Block())

        @block.sync
        def _(sp):
            def load(b):
                coming = channel_tiles(y[b])
                if needed(CT * b):
                    sp.wait_ge(centred, CT * b)
                sp.dma_start(y_in[:], coming).then_inc(y_loaded, DMA)

            sp.dma_start(vecs[:], vectors).then_inc(vectors_in, DMA)
            sp.dma_start(tap[:], taps.rearrange("(t p) k -> p t k", p=P)).then_inc(vectors_in, DMA)
            load(0)
            for dst, src in ((fc1_f, channel_tiles(fc1)), (fc2_f, channel_tiles(fc2T)), (w_f, channel_tiles(wqkvT)),
                             (kvb[:], kv_bias.unsqueeze(0).broadcast_to([P, 2 * C]))):
                sp.dma_start(dst, src).then_inc(w_in, DMA)
            sp.wait_ge(v_inited, 1)
            sp.dma_start(k_in[PAD:P, NT - 1, :], kv_bias[0:C].unsqueeze(0)).then_inc(w_in, DMA)
            sp.dma_start(v1[PAD:P, NT - 1, :, 0:P],
                         kv_bias[C:].rearrange("(t d) -> t d", t=CT).unsqueeze(0)).then_inc(w_in, DMA)

            def store(b):
                sp.wait_ge(out_ready, ORDERS * CT * (b + 1))
                sp.dma_start(channel_tiles(out[b]), res[:]).then_inc(out_sent, DMA)

            load(1)

            def image(b, p, sl, first=False, last=False):
                if not isinstance(b, int) or b + 2 < B:
                    load(b + 2)
                if not first:
                    store(b - 1)

            for_images(sp, image)
            store(B - 1)
            sp.wait_ge(out_sent, DMA * B)

        @block.tensor
        def _(pe):
            def product(o, left, right):
                terms = [(l, r) for (lu, ll), (ru, rl) in zip(left, right) for l, r in ((lu, ru), (lu, rl), (ll, ru))]
                for n, (l, r) in enumerate(terms):
                    mm = nc.tensor.matmul(o, l, r, start=(n == 0), stop=(n == len(terms) - 1))
                return mm

            pe.wait_ge(vectors_in, 2 * DMA)
            pe.wait_ge(w_in, 6 * DMA)
            for m in range(CT):
                for f in range(FT):
                    mm = nc.tensor.matmul(early[m][:, 0:C], fc1_f[:, f, m * P:(m + 1) * P], fc2_f[:, f, :],
                                          start=(f == 0), stop=(f == FT - 1))
            for m in range(CT):
                for f in range(FT):
                    mm = nc.tensor.matmul(early[2][:, m:m + 1], fc2_f[:, f, m * P:(m + 1) * P], fc1_b[:, f:f + 1],
                                          start=(f == 0), stop=(f == FT - 1))
            mm.then_inc(mlp_made, 1)
            pe.wait_ge(w_ready, 1)
            pe.wait_ge(consts, 1)

            def q_products(sl, b, t):
                pe.wait_ge(x1_l_ready, CT * (b + 1))
                to = sl["q", t]
                if needed(to.emptied):
                    pe.wait_ge(to.free, to.emptied)
                o = to.tile
                m = slice(t * P, (t + 1) * P)
                for n in halves:
                    mm = product(o[:, n], [(w_u[:, k, m], w_l[:, k, m]) for k in range(CT)],
                                 [(x1_u[:, k, n], x1_l[:, k, n]) for k in range(CT)])
                mm.then_inc(to.full, 1)

            def kv_products(sl, b, u):
                pe.wait_ge(x1_l_ready, CT * (b + 1))
                to = sl["kv", u]
                if needed(to.emptied):
                    pe.wait_ge(to.free, to.emptied)
                o = to.tile
                for i, (_, first_, tokens) in enumerate(TILES[2 * u:2 * u + 2]):
                    n = slice(first_, first_ + tokens)
                    mm = product(o[0:tokens, i * HALF:(i + 1) * HALF],
                                 [(x1_u[:, k, n], x1_l[:, k, n]) for k in range(CT)],
                                 [(w_u[:, k, C:], w_l[:, k, C:]) for k in range(CT)])
                mm.then_inc(to.full, 1)

            def square_sums(sl, b, t):
                pe.wait_ge(q_f_ready, 2 * CT * b + 2 * t + 2)
                to = sl["norm", t]
                if needed(to.emptied):
                    pe.wait_ge(to.free, to.emptied)
                o = to.tile
                for n in halves:
                    mm = nc.tensor.matmul(o[:, n], head_ones[:], q_w[:, t, n], start=True, stop=True)
                mm.then_inc(to.full, 1)

            def state(sl, b, u):
                pe.wait_ge(k_s_ready, b + 1)
                pe.wait_ge(v_split, b + 1)
                to = sl["state", u]
                if needed(to.emptied):
                    pe.wait_ge(to.free, to.emptied)
                o = to.tile
                for cell in range(6 * u, 6 * u + 6):
                    t, w = divmod(cell, NW)
                    at_ = cell % 6 // 3 * HALF + cell % 3 * (P + 2)
                    mine = ([(n, v1[:, n, t, :]) for n in (2 * w, 2 * w + 1)] if w < WHOLE
                            else [(NT - 1, v_cut[:, w - WHOLE, t, :])])
                    for i, (n, v) in enumerate(mine):
                        mm = nc.tensor.matmul(o[:, at_:at_ + P + 2], k_w[:, n, t * P:(t + 1) * P], v,
                                              start=(i == 0), stop=(i == len(mine) - 1))
                mm.then_inc(to.full, 1)

            def attend(sl, images, name, table, t):
                pe.wait_ge(q_s_ready, CT * images)
                pe.wait_ge(kv_ready, 9 * images)
                to = sl[name, t]
                if needed(to.emptied):
                    pe.wait_ge(to.free, to.emptied)
                for w, (at_, tokens) in enumerate(WINDOWS):
                    cuts = sorted({at_, min(max(HALF, at_), at_ + tokens), at_ + tokens})
                    for a, c in zip(cuts, cuts[1:]):
                        mm = nc.tensor.matmul(to.tile[:, a:c], table[:, t * NW + w, :], q_s[:, t, a:c],
                                              start=True, stop=True)
                mm.then_inc(to.full, 1)

            def mlp(sl, images, m):
                pe.wait_ge(x2_l_ready, CT * images)
                to = sl["mlp", m]
                if needed(to.emptied):
                    pe.wait_ge(to.free, to.emptied)
                o = to.tile
                mm_ = slice(m * P, (m + 1) * P)
                for n in halves:
                    mm = product(o[:, n], [(m_u[:, k, mm_], m_l[:, k, mm_]) for k in range(CT)],
                                 [(x2_u[:, k, n], x2_l[:, k, n]) for k in range(CT)])
                mm.then_inc(to.full, 1)

            def image(b, p, sl, first=False, last=False):
                for what, i in products1(first):
                    if what == "q":
                        q_products(sl, b, i)
                    elif what == "kv":
                        kv_products(sl, b, i)
                    elif what == "norm":
                        square_sums(sl, b, i)
                    elif what == "state":
                        state(sl, b, i)
                    elif what == "mlp":
                        mlp(sl, b, i)
                    else:
                        attend(sl, b, what, ks if what == "den" else kv, i)

            for_images(pe, image)
            for what, table in (("den", ks), ("num", kv)):
                for t in range(CT):
                    attend(tail_slots, B, what, table, t)
            for m in range(CT):
                mlp(tail_slots, B, m)

        @block.scalar
        def _(act):
            def prepare(b, t):
                act.wait_ge(y_loaded, DMA * (b + 1))
                if needed(8 * b):
                    act.wait_ge(tapped[t], 8 * b)
                nc.scalar.copy(y_pad[:, t, 1:SIDE + 1, 1:SIDE + 1], image_view(y_in[:, t, :])).then_inc(padded, 1)
                if needed(ORDERS * (CT * (b - 1) + t + 1)):
                    act.wait_ge(ordered, ORDERS * (CT * (b - 1) + t + 1))
                nc.scalar.activation(x1[:, t, :], y_in[:, t, :], ACT.Identity, scale=centre[:, t:t + 1],
                                     bias=conv_b[:, t:t + 1]).then_inc(centred, 1)

            def upper_x1(b, p, sl, t):
                act.wait_ge(tapped[t], 8 * (b + 1))
                if needed(CT * (b - 1)):
                    act.wait_ge(x2_ready, CT * (b - 1))
                for image_, windows in orders(x1[:, t, :], x1w[p][:, t, :]):
                    nc.scalar.copy(windows, image_).then_inc(ordered, 1)
                act.wait_ge(ordered, ORDERS * (CT * b + t + 1))
                if sl is not None:
                    it = sl["kv", (NT - 1) // 2]
                    act.wait_ge(it.free, it.filled)
                nc.scalar.copy(x1_u[:, t, :], x1w[p][:, t, :]).then_inc(x1_u_ready, 1)

            def q_parts(sl, b, t):
                it = sl["q", t]
                act.wait_ge(it.full, it.filled)
                src = it.tile
                if needed(CT * b):
                    act.wait_ge(q_n, CT * b)
                nc.scalar.activation(q_f[:, t, :], src[:], ACT.Identity, bias=q_bias[:, t:t + 1]).then_inc(q_f_ready, 1)
                if needed(CT * b):
                    act.wait_ge(q_s_ready, CT * b)
                nc.scalar.activation(q_w[:, t, :], src[:], ACT.Square, bias=q_bias[:, t:t + 1]).then_inc(q_f_ready, 1)
                act.wait_ge(q_f_ready, 2 * CT * b + 2 * t + 2)
                act.sem_inc(it.free, 1)

            def q_ln_norm(sl, b, t):
                it = sl["norm", t]
                act.wait_ge(it.full, it.filled)
                nc.scalar.activation(q_w[:, t, :], it.tile[:], ACT.Ln, scale=LIFT, bias=tiny[:]).then_inc(q_ln, 1)
                act.wait_ge(q_ln, CT * b + t + 1)
                act.sem_inc(it.free, 1)

            def q_rnorm(b, t):
                act.wait_ge(q_clamped, CT * b + t + 1)
                nc.scalar.activation(q_w[:, t, :], q_w[:, t, :], ACT.Exp, scale=-0.5, bias=unlift[:]).then_inc(q_rn, 1)

            def q_softplus(sl, b, t, first):
                act.wait_ge(q_n, CT * b + t + 1)
                nc.scalar.activation(q_w[:, t, :], q_w[:, t, :], ACT.Exp).then_inc(q_exp, 1)
                act.wait_ge(q_exp, CT * b + t + 1)
                if not first:
                    it = sl["num", t]
                    act.wait_ge(it.full, it.filled)
                nc.scalar.activation(q_s[:, t, :], q_w[:, t, :], ACT.Ln, bias=1.0).then_inc(q_s_ready, 1)

            def k_square(sl, b):
                act.wait_ge(k_added, NT * (b + 1))
                if needed(9 * b):
                    act.wait_ge(kv_ready, 9 * b)
                nc.scalar.activation(k_w[:], k_in[:], ACT.Square).then_inc(k_step, 1)

            def k_rnorm(b):
                act.wait_ge(k_rn, 6 * b + 2)
                nc.scalar.activation(kln[:], ksq[:], ACT.Ln, scale=LIFT).then_inc(k_step, 1)
                act.wait_ge(k_step, 4 * b + 2)
                nc.scalar.activation(krn[:], kln[:], ACT.Exp, scale=-0.5, bias=unlift[:]).then_inc(k_step, 1)

            def k_softplus(b):
                act.wait_ge(k_rn, 6 * b + 6)
                nc.scalar.activation(k_w[:], k_w[:], ACT.Exp).then_inc(k_step, 1)
                act.wait_ge(k_step, 4 * b + 4)
                nc.scalar.activation(k_w[:], k_w[:], ACT.Ln, bias=1.0).then_inc(k_s_ready, 1)

            def reciprocal(sl, images, t):
                it = sl["den", t]
                act.wait_ge(it.full, it.filled)
                if needed(ORDERS * CT * (images - 1)):
                    act.wait_ge(out_ready, ORDERS * CT * (images - 1))
                nc.scalar.activation(x2[:, t, :], it.tile[:], ACT.Ln).then_inc(it.free, 1)
                it = sl["den", t]
                act.wait_ge(it.free, it.filled)
                nc.scalar.activation(x2[:, t, :], x2[:, t, :], ACT.Exp, scale=-1.0).then_inc(rec_ready, 1)

            def upper_x2(images, t):
                act.wait_ge(x2_ready, CT * (images - 1) + t + 1)
                nc.scalar.copy(x2_u[:, t, :], x2[:, t, :]).then_inc(x2_u_ready, 1)

            def reorder(sl, images, m):
                if needed(DMA * (images - 1)):
                    act.wait_ge(out_sent, DMA * (images - 1))
                it = sl["mlp", m]
                act.wait_ge(it.free, it.filled)
                for image_, windows in orders(res[:, m, :], x2[:, m, :]):
                    nc.scalar.copy(image_, windows).then_inc(out_ready, 1)

            nc.scalar.preload_act_table_set("natural_log_exp_and_others")
            act.wait_ge(vectors_in, 2 * DMA)
            act.wait_ge(centre_made, 1)
            act.wait_ge(framed, 1)
            for t in range(CT):
                prepare(0, t)
            for t in range(CT):
                upper_x1(0, 0, None, t)
            act.wait_ge(consts, 1)

            def image(b, p, sl, first=False, last=False):
                if not last:
                    prepare(b + 1, 0)
                    prepare(b + 1, 1)
                q_parts(sl, b, 0)
                q_parts(sl, b, 1)
                k_square(sl, b)
                q_ln_norm(sl, b, 0)
                if not first:
                    reciprocal(sl, b, 0)
                q_ln_norm(sl, b, 1)
                k_rnorm(b)
                q_rnorm(b, 0)
                if not first:
                    reciprocal(sl, b, 1)
                k_softplus(b)
                if not first:
                    upper_x2(b, 0)
                    upper_x2(b, 1)
                q_softplus(sl, b, 0, first)
                q_rnorm(b, 1)
                if not last:
                    upper_x1(b + 1, 1 - p, sl, 0)
                    upper_x1(b + 1, 1 - p, sl, 1)
                q_softplus(sl, b, 1, first)
                if not first:
                    reorder(sl, b, 0)
                    reorder(sl, b, 1)
            for_images(act, image)
            for t in range(CT):
                reciprocal(tail_slots, B, t)
            for t in range(CT):
                upper_x2(B, t)
            for m in range(CT):
                reorder(tail_slots, B, m)

        @block.vector
        def _(dve):
            def convolve(b, taps_):
                around = [(dy, dx) for dy in range(3) for dx in range(3) if (dy, dx) != (1, 1)]
                for n in taps_:
                    dy, dx = around[n]
                    for t in range(CT):
                        if n == 0:
                            dve.wait_ge(centred, CT * b + t + 1)
                        else:
                            dve.wait_ge(tapped[t], 8 * b + n)
                        nc.vector.scalar_tensor_tensor(
                            out=image_view(x1[:, t, :]), in0=y_pad[:, t, dy:dy + SIDE, dx:dx + SIDE],
                            scalar=tap[:, t, 3 * dy + dx:3 * dy + dx + 1], in1=image_view(x1[:, t, :]), op0=ALU.mult,
                            op1=ALU.add).then_inc(tapped[t], 1)

            def add_bias(sl, b, u):
                it = sl["kv", u]
                dve.wait_ge(it.full, it.filled)
                src = it.tile
                tiles = list(enumerate(TILES))[2 * u:2 * u + 2]
                for i, (n, (_, _, tokens)) in enumerate(tiles):
                    at_ = i * HALF
                    nc.vector.tensor_tensor(k_in[0:tokens, n, :], src[0:tokens, at_:at_ + C], kvb[0:tokens, 0:C],
                                            ALU.add).then_inc(k_added, 1)
                    nc.vector.tensor_tensor(
                        v1[0:tokens, n, :, 0:P], src[0:tokens, at_ + C:at_ + 2 * C].rearrange("p (t d) -> p t d", t=CT),
                        kvb[0:tokens, C:].rearrange("p (t d) -> p t d", t=CT), ALU.add).then_inc(
                            it.free if i == len(tiles) - 1 else v_added, 1)

            def split_v(sl, b):
                it = sl["kv", (NT - 1) // 2]
                dve.wait_ge(it.free, it.filled)
                shape = [P, len(CUT), CT * (P + 2)]
                nc.vector.tensor_tensor(
                    v_cut[:].rearrange("p w t d -> p w (t d)"),
                    v1[:, NT - 1, :, :].rearrange("p t d -> p (t d)").unsqueeze(1).broadcast_to(shape),
                    cut_mask[:].unsqueeze(2).broadcast_to(shape), ALU.mult).then_inc(v_split, 1)

            def k_norms(b):
                n = 6 * b
                dve.wait_ge(k_step, 4 * b + 1)
                nc.vector.tensor_reduce(ksq[:], k_w[:].rearrange("p n (h d) -> p (n h) d", d=HD), AX.X,
                                        ALU.add).then_inc(k_rn, 1)
                dve.wait_ge(k_rn, n + 1)
                nc.vector.tensor_scalar(ksq[:], ksq[:], NORM_MIN ** 2, None, ALU.max).then_inc(k_rn, 1)

            def k_normalise(b):
                n = 6 * b
                dve.wait_ge(k_step, 4 * b + 3)
                nc.vector.tensor_tensor(knw[:], krn[:], ksq[:], ALU.mult).then_inc(k_rn, 1)
                dve.wait_ge(k_rn, n + 3)
                nc.vector.tensor_tensor(knw[:], knw[:], krn[:], ALU.mult).then_inc(k_rn, 1)
                dve.wait_ge(k_rn, n + 4)
                nc.vector.tensor_scalar(knw[:], knw[:], -0.5, 1.5, ALU.mult, ALU.add).then_inc(k_n, 1)
                dve.wait_ge(k_n, 2 * b + 1)
                nc.vector.tensor_tensor(knw[:], knw[:], krn[:], ALU.mult).then_inc(k_n, 1)
                dve.wait_ge(k_n, 2 * b + 2)
                by_head = k_w[:].rearrange("p n (h d) -> p (n h) d", d=HD)
                nc.vector.tensor_tensor(by_head, k_in[:].rearrange("p n (h d) -> p (n h) d", d=HD),
                                        knw[:].unsqueeze(2).broadcast_to([P, NT * HEADS1, HD]), ALU.mult).then_inc(k_rn, 1)
                dve.wait_ge(k_rn, n + 5)
                dve.sem_inc(k_rn, 1)

            def tables(sl, b, u):
                it = sl["state", u]
                dve.wait_ge(it.full, it.filled)
                src = it.tile
                cells = src[:].rearrange("p (a n) -> p a n", a=2)[:, :, 0:3 * (P + 2)].rearrange(
                    "p a (w e) -> p a w e", e=P + 2)
                shape = [P, 2, 3, P]

                def by_cell(tile):
                    return tile[:, 6 * u:6 * u + 6, :].rearrange("p (a w) e -> p a w e", w=3)

                def mask(tile):
                    return tile[:].unsqueeze(1).unsqueeze(1).broadcast_to(shape)

                nc.vector.tensor_tensor(by_cell(kv), cells[:, :, :, 0:P], mask(head_scale), ALU.mult).then_inc(kv_ready, 1)
                for a in range(2):
                    nc.vector.scalar_tensor_tensor(
                        out=by_cell(ks)[:, a], in0=cells[:, a, :, P:P + 1].broadcast_to([P, 3, P]), scalar=EPS,
                        in1=head_ones[:].unsqueeze(1).broadcast_to([P, 3, P]), op0=ALU.add,
                        op1=ALU.mult).then_inc(kv_ready, 1)
                dve.wait_ge(kv_ready, 9 * b + 3 * u + 3)
                dve.sem_inc(it.free, 1)

            def weighted(sl, images, t):
                dve.wait_ge(rec_ready, CT * (images - 1) + t + 1)
                it = sl["num", t]
                dve.wait_ge(it.full, it.filled)
                nc.vector.tensor_tensor(x2[:, t, :], it.tile[:], x2[:, t, :], ALU.mult).then_inc(it.free, 1)

            def finish(sl, images, m):
                it = sl["mlp", m]
                dve.wait_ge(it.full, it.filled)
                src = it.tile
                nc.vector.scalar_tensor_tensor(out=x2[:, m, :], in0=src[:], scalar=mlp_bias[:, m:m + 1], in1=x2[:, m, :],
                                               op0=ALU.add, op1=ALU.add).then_inc(it.free, 1)

            dve.wait_ge(vectors_in, 2 * DMA)
            nc.vector.tensor_scalar(centre[:], tap[:, :, 4], 1.0, None, ALU.add).then_inc(centre_made, 1)
            convolve(0, range(4))
            dve.wait_ge(w_in, 6 * DMA)
            nc.vector.tensor_copy(w_u[:], w_f).then_inc(w_split, 1)
            dve.wait_ge(w_split, 1)
            nc.vector.tensor_tensor(w_l[:], w_f, w_u[:].bitcast(F32), ALU.subtract).then_inc(w_split, 1)
            convolve(0, range(4, 8))
            dve.wait_ge(mlp_made, 1)
            for m in range(CT):
                nc.vector.tensor_copy(m_u[:, m, :], early[m][:, 0:C]).then_inc(w_split, 1)
            dve.wait_ge(w_split, 4)
            for m in range(CT):
                nc.vector.tensor_tensor(m_l[:, m, :], early[m][:, 0:C], m_u[:, m, :].bitcast(F32),
                                        ALU.subtract).then_inc(w_split, 1)
            nc.vector.tensor_tensor(mlp_bias[:], early[2][:, 0:CT], fc2_b, ALU.add).then_inc(w_split, 1)
            dve.wait_ge(w_split, 7)
            dve.sem_inc(w_ready, 1)

            def image(b, p, sl, first=False, last=False):
                add_bias(sl, b, 0)
                if not last:
                    convolve(b + 1, (0,))
                add_bias(sl, b, 1)
                if not last:
                    convolve(b + 1, (1, 2))
                add_bias(sl, b, 2)
                if not last:
                    convolve(b + 1, (3,))
                add_bias(sl, b, 3)
                add_bias(sl, b, 4)
                if not last:
                    convolve(b + 1, (4,))
                k_norms(b)
                split_v(sl, b)
                k_normalise(b)
                if not first:
                    weighted(sl, b, 0)
                    weighted(sl, b, 1)
                if not last:
                    convolve(b + 1, (5, 6, 7))
                tables(sl, b, 0)
                tables(sl, b, 1)
                if not first:
                    finish(sl, b, 0)
                    finish(sl, b, 1)
                tables(sl, b, 2)
            for_images(dve, image)
            for t in range(CT):
                weighted(tail_slots, B, t)
            for m in range(CT):
                finish(tail_slots, B, m)

        @block.gpsimd
        def _(pool):
            made = [0]

            def const(instruction):
                made[0] += 1
                instruction.then_inc(c_step, 1)
                pool.wait_ge(c_step, made[0])

            const(nc.gpsimd.memset(y_pad[:], 0.0))
            pool.sem_inc(framed, 1)
            const(nc.gpsimd.memset(k_in[:], 0.0))
            const(nc.gpsimd.memset(v1[:], 0.0))
            for n, (_, _, tokens) in enumerate(TILES):
                rows = P if n == NT - 1 else tokens
                const(nc.gpsimd.memset(v1[0:rows, n, :, P:P + 1], 1.0))
            const(nc.gpsimd.memset(cut_mask[:], 1.0))
            for base, step, row in ((0, -WS * EDGE, 1), (WS * EDGE - 1, WS * EDGE, -1), (sum(CUT) - 1, 0, -1)):
                const(nc.gpsimd.affine_select(out=cut_mask[:], in_=cut_mask[:], compare_op=ALU.is_ge, fill=0.0, base=base,
                                              pattern=[[step, len(CUT)]], channel_multiplier=row))
            for i, size in enumerate(CUT):
                column = cut_mask[:, i:i + 1]
                const(nc.gpsimd.affine_select(out=column, in_=column, compare_op=ALU.not_equal, fill=float(WS * WS - size),
                                              base=-PAD, pattern=[[0, 1]], channel_multiplier=1))
            pool.sem_inc(v_inited, 1)
            for tile, value in ((head_ones, 1.0), (head_scale, SCALE)):
                const(nc.gpsimd.memset(tile[:], value))
                v = tile[:].rearrange("p (g c) -> p g c", c=HD)
                const(nc.gpsimd.affine_select(out=v, in_=v, compare_op=ALU.is_ge, fill=0.0, base=0,
                                              pattern=[[-HD, P // HD], [0, HD]], channel_multiplier=1))
                const(nc.gpsimd.affine_select(out=v, in_=v, compare_op=ALU.is_ge, fill=0.0, base=HD - 1,
                                              pattern=[[HD, P // HD], [0, HD]], channel_multiplier=-1))
            const(nc.gpsimd.memset(unlift[:], 0.5 * math.log(LIFT)))
            const(nc.gpsimd.memset(tiny[:], 1e-30))
            pool.sem_inc(consts, 1)

            def clamp_q(b, t):
                pool.wait_ge(q_ln, CT * b + t + 1)
                pool.sem_inc(waited, 1)
                nc.gpsimd.tensor_scalar(q_w[:, t, :], q_w[:, t, :], math.log(NORM_MIN ** 2 * LIFT), None,
                                        ALU.max).then_inc(q_clamped, 1)

            def normalise_q(b, t):
                n = CT * b + t
                pool.wait_ge(q_rn, n + 1)
                nc.gpsimd.tensor_tensor(q_w[:, t, :], q_f[:, t, :], q_w[:, t, :], ALU.mult).then_inc(q_n, 1)

            def add_attention(sl, p, t):
                it = sl["num", t]
                pool.wait_ge(it.free, it.filled)
                nc.gpsimd.tensor_tensor(x2[:, t, :], x1w[p][:, t, :], x2[:, t, :], ALU.add).then_inc(x2_ready, 1)

            def lower_x1(b, p, t):
                pool.wait_ge(x1_u_ready, CT * b + t + 1)
                nc.gpsimd.tensor_tensor(x1_l[:, t, :], x1w[p][:, t, :], x1_u[:, t, :].bitcast(F32),
                                        ALU.subtract).then_inc(x1_l_ready, 1)

            def lower_x2(images, t):
                pool.wait_ge(x2_u_ready, CT * (images - 1) + t + 1)
                nc.gpsimd.tensor_tensor(x2_l[:, t, :], x2[:, t, :], x2_u[:, t, :].bitcast(F32),
                                        ALU.subtract).then_inc(x2_l_ready, 1)

            for t in range(CT):
                lower_x1(0, 0, t)

            def image(b, p, sl, first=False, last=False):
                clamp_q(b, 0)
                clamp_q(b, 1)
                normalise_q(b, 0)
                if not first:
                    add_attention(sl, 1 - p, 0)
                    add_attention(sl, 1 - p, 1)
                    lower_x2(b, 0)
                    lower_x2(b, 1)
                normalise_q(b, 1)
                if not last:
                    lower_x1(b + 1, 1 - p, 0)
                    lower_x1(b + 1, 1 - p, 1)
            for_images(pool, image)
            for t in range(CT):
                add_attention(tail_slots, (B - 1) % 2, t)
            for t in range(CT):
                lower_x2(B, t)


def program(nc, x, vectors0, qkv_wT, p_wT, vectors1, taps, wqkvT, kv_bias, fc1, fc2T, out):
    y = nc.dram_tensor("layer0_out", x.shape, F32).ap()
    layer0(nc, x, vectors0, qkv_wT, p_wT, y)
    layer1(nc, y, vectors1, taps, wqkvT, kv_bias, fc1, fc2T, out)


def kernel(**inputs):
    import numpy as _np
    import concourse.bacc as _bacc
    from concourse import mybir as _mybir
    from concourse.bass_utils import run_bass_kernel_spmd as _run

    a = {name: _np.asarray(value) for name, value in inputs.items()}
    B, C, H, W = a["x"].shape

    def columns(*names):
        return _np.ascontiguousarray(_np.concatenate([a[n].reshape(-1, P) for n in names]).T)

    wqkv, bqkv = a["L1_conv_wqkv"], a["L1_conv_bqkv"]
    a["q_bias"] = bqkv[:C]
    arrays = {
        "x": _np.ascontiguousarray(a["x"].reshape(B, C, H * W)),
        "vectors0": columns("L0_conv_n_weight", "L0_conv_n_bias", "L0_conv_p_b", "L0_conv_qkv_b"),
        "qkv_wT": _np.ascontiguousarray(a["L0_conv_qkv_w"].T),
        "p_wT": _np.ascontiguousarray(a["L0_conv_p_w"].T),
        "vectors1": columns("L1_conv_conv_b", "q_bias", "L1_conv_bfc2", "L1_conv_bfc1"),
        "taps": _np.ascontiguousarray(a["L1_conv_conv_w"].reshape(C, 9)),
        "wqkvT": _np.ascontiguousarray(wqkv.T),
        "kv_bias": _np.ascontiguousarray(bqkv[C:]),
        "fc1": _np.ascontiguousarray(a["L1_conv_wfc1"]),
        "fc2T": _np.ascontiguousarray(a["L1_conv_wfc2"].T),
    }
    nc = _bacc.Bacc("TRN2", target_bir_lowering=False, num_devices=1)
    args = [nc.dram_tensor(f"in_{name}", v.shape, _mybir.dt.from_np(v.dtype), kind="ExternalInput").ap()
            for name, v in arrays.items()]
    args.append(nc.dram_tensor("out_0", (B, C, H * W), F32, kind="ExternalOutput").ap())
    program(nc, *args)
    r = _run(nc, [{f"in_{name}": v for name, v in arrays.items()}], core_ids=[0])
    return r.results[0]["out_0"].reshape(B, C, H, W)
```
